# Optimizing a Trainium2 kernel written in Bass

```python
import numpy as np
import jax
import jax.numpy as jnp

def _softmax(x, axis=-1):
    return jax.nn.softmax(x, axis=axis)

def _gelu(x):
    return jax.nn.gelu(x, approximate=True)

def _silu(x):
    return jax.nn.silu(x)

def _sigmoid(x):
    return jax.nn.sigmoid(x)

def _layernorm(x, axis=-1, eps=1e-05):
    m = jnp.mean(x, axis=axis, keepdims=True)
    v = jnp.var(x, axis=axis, keepdims=True)
    return (x - m) / jnp.sqrt(v + eps)

def _scatter_add(tgt, idx, src, axis=0):
    return tgt.at[idx].add(src)

def _segment_sum(src, seg, n):
    return jax.ops.segment_sum(src, seg, n)
kernel_name = 'mk_adj_preln_d2_adj_r2_5f3689'

def setup_inputs(seed: int=0):
    np.random.seed(seed)
    _w = jnp.asarray

    def _rec_inputs():
        import jax
        import jax.numpy as jnp
        _gk = jax.random.key(seed)
        x = -2.603e-05 + 0.05003 * jax.random.normal(jax.random.fold_in(_gk, 1), (4096, 128), jnp.float32)
        _w = (1.0 + jnp.arange(4096, dtype=jnp.float32)) ** (-0.5)
        _w = _w / _w.mean()
        _pij = jnp.clip(0.00390625 * _w[:, None] * _w[None, :], 0.0, 1.0)
        _a = jax.random.uniform(jax.random.fold_in(_gk, 2), (4096, 4096)) < _pij
        _a = jnp.logical_or(_a, jnp.eye(4096, dtype=bool))
        _af = _a.astype(jnp.float32)
        _af = _af / jnp.maximum(_af.sum(-1, keepdims=True), 1.0)
        adj = _af
        return (x, adj)
    x, adj = _rec_inputs()

    def _L0_gnn_setup():
        import jax, jax.numpy as jnp
        import numpy as np
        MIN_NORM = 1e-15
        BALL_EPS = 1e-05
        C_IN = 1.0
        C_OUT = 1.0

        def _artanh(x):
            x = jnp.clip(x, -1.0 + 1e-07, 1.0 - 1e-07)
            return 0.5 * (jnp.log1p(x) - jnp.log1p(-x))

        def _norm(x):
            return jnp.maximum(jnp.linalg.norm(x, axis=-1, keepdims=True), MIN_NORM)

        def proj(x, c):
            norm = _norm(x)
            maxnorm = (1.0 - BALL_EPS) / jnp.sqrt(c)
            return jnp.where(norm > maxnorm, x / norm * maxnorm, x)

        def expmap0(u, c):
            sc = jnp.sqrt(c)
            un = _norm(u)
            return jnp.tanh(sc * un) * u / (sc * un)

        def logmap0(p, c):
            sc = jnp.sqrt(c)
            pn = _norm(p)
            return _artanh(sc * pn) * p / (sc * pn)

        def mobius_matvec(m, x, c):
            sc = jnp.sqrt(c)
            xn = _norm(x)
            mx = x @ m.T
            mxn = _norm(mx)
            res = jnp.tanh(mxn / xn * _artanh(sc * xn)) * mx / (mxn * sc)
            zero_row = jnp.all(mx == 0, axis=-1, keepdims=True)
            return jnp.where(zero_row, jnp.zeros((), dtype=res.dtype), res)

        def mobius_add(x, y, c):
            x2 = jnp.sum(x * x, axis=-1, keepdims=True)
            y2 = jnp.sum(y * y, axis=-1, keepdims=True)
            xy = jnp.sum(x * y, axis=-1, keepdims=True)
            num = (1.0 + 2.0 * c * xy + c * y2) * x + (1.0 - c * x2) * y
            denom = 1.0 + 2.0 * c * xy + c * c * x2 * y2
            return num / jnp.maximum(denom, MIN_NORM)
        key = jax.random.key(seed)
        k1, k2, k3, k4 = jax.random.split(key, 4)
        N, D_IN, D_OUT = (4096, 128, 128)
        x = proj(0.05 * jax.random.normal(k1, (N, D_IN), dtype=jnp.float32), C_IN)
        adj = jax.random.uniform(k2, (N, N), dtype=jnp.float32)
        adj = adj / jnp.sum(adj, axis=1, keepdims=True)
        bound = np.sqrt(2.0) * np.sqrt(6.0 / (D_IN + D_OUT))
        weight = jax.random.uniform(k3, (D_OUT, D_IN), dtype=jnp.float32, minval=-bound, maxval=bound)
        bias = 0.01 * jax.random.normal(k4, (D_OUT,), dtype=jnp.float32)
        return {'x': x, 'adj': adj, 'weight': weight, 'bias': bias}
    _L0_gnn_all = _L0_gnn_setup()
    _L0_gnn_in = {k: v for k, v in _L0_gnn_all.items() if k in ('weight', 'bias')}
    del _L0_gnn_all

    def _L1_gnn_setup():
        import jax, jax.numpy as jnp
        import numpy as np
        N = 4096
        IN_DIM = 256
        HID = 128
        REL_DIM = 128
        key = jax.random.key(seed)
        ks = jax.random.split(key, 8)
        s = 1.0 / np.sqrt(IN_DIM)
        return {'relation': jax.random.normal(ks[0], (N, REL_DIM), dtype=jnp.float32), 'context': jax.random.normal(ks[1], (N, IN_DIM), dtype=jnp.float32), 'adj_tensor': jax.random.randint(ks[2], (N, N), 0, 2).astype(jnp.float32), 'W_common': jax.random.normal(ks[3], (HID, IN_DIM), dtype=jnp.float32) * s, 'w_left': jax.random.normal(ks[4], (HID,), dtype=jnp.float32) * (1.0 / np.sqrt(HID)), 'b_left': jax.random.normal(ks[5], (), dtype=jnp.float32) * 0.01, 'w_right': jax.random.normal(ks[6], (HID,), dtype=jnp.float32) * (1.0 / np.sqrt(HID)), 'b_right': jax.random.normal(ks[7], (), dtype=jnp.float32) * 0.01}
    _L1_gnn_all = _L1_gnn_setup()
    _L1_gnn_in = {k: v for k, v in _L1_gnn_all.items() if k in ('context', 'W_common', 'w_left', 'b_left', 'w_right', 'b_right')}
    del _L1_gnn_all
    return {'x': x, 'adj': adj, 'L0_gnn_weight': _L0_gnn_in['weight'], 'L0_gnn_bias': _L0_gnn_in['bias'], 'L1_gnn_context': _L1_gnn_in['context'], 'L1_gnn_W_common': _L1_gnn_in['W_common'], 'L1_gnn_w_left': _L1_gnn_in['w_left'], 'L1_gnn_b_left': _L1_gnn_in['b_left'], 'L1_gnn_w_right': _L1_gnn_in['w_right'], 'L1_gnn_b_right': _L1_gnn_in['b_right']}

def reference(x, adj, L0_gnn_weight, L0_gnn_bias, L1_gnn_context, L1_gnn_W_common, L1_gnn_w_left, L1_gnn_b_left, L1_gnn_w_right, L1_gnn_b_right):
    import jax
    import jax.numpy as jnp

    def _L0_gnn_ref(x, adj, weight, bias):
        import jax, jax.numpy as jnp
        import numpy as np
        MIN_NORM = 1e-15
        BALL_EPS = 1e-05
        C_IN = 1.0
        C_OUT = 1.0

        def _artanh(x):
            x = jnp.clip(x, -1.0 + 1e-07, 1.0 - 1e-07)
            return 0.5 * (jnp.log1p(x) - jnp.log1p(-x))

        def _norm(x):
            return jnp.maximum(jnp.linalg.norm(x, axis=-1, keepdims=True), MIN_NORM)

        def proj(x, c):
            norm = _norm(x)
            maxnorm = (1.0 - BALL_EPS) / jnp.sqrt(c)
            return jnp.where(norm > maxnorm, x / norm * maxnorm, x)

        def expmap0(u, c):
            sc = jnp.sqrt(c)
            un = _norm(u)
            return jnp.tanh(sc * un) * u / (sc * un)

        def logmap0(p, c):
            sc = jnp.sqrt(c)
            pn = _norm(p)
            return _artanh(sc * pn) * p / (sc * pn)

        def mobius_matvec(m, x, c):
            sc = jnp.sqrt(c)
            xn = _norm(x)
            mx = x @ m.T
            mxn = _norm(mx)
            res = jnp.tanh(mxn / xn * _artanh(sc * xn)) * mx / (mxn * sc)
            zero_row = jnp.all(mx == 0, axis=-1, keepdims=True)
            return jnp.where(zero_row, jnp.zeros((), dtype=res.dtype), res)

        def mobius_add(x, y, c):
            x2 = jnp.sum(x * x, axis=-1, keepdims=True)
            y2 = jnp.sum(y * y, axis=-1, keepdims=True)
            xy = jnp.sum(x * y, axis=-1, keepdims=True)
            num = (1.0 + 2.0 * c * xy + c * y2) * x + (1.0 - c * x2) * y
            denom = 1.0 + 2.0 * c * xy + c * c * x2 * y2
            return num / jnp.maximum(denom, MIN_NORM)
        h = proj(mobius_matvec(weight, x, C_IN), C_IN)
        hyp_bias = proj(expmap0(bias[None, :], C_IN), C_IN)
        h = proj(mobius_add(h, hyp_bias, C_IN), C_IN)
        x_tangent = logmap0(h, C_IN)
        support_t = adj @ x_tangent
        h = proj(expmap0(support_t, C_IN), C_IN)
        xt = jax.nn.relu(logmap0(h, C_IN))
        return proj(expmap0(xt, C_OUT), C_OUT)

    def _L1_gnn_ref(relation, context, adj_tensor, W_common, w_left, b_left, w_right, b_right):
        import jax, jax.numpy as jnp
        import numpy as np
        N = 4096
        IN_DIM = 256
        HID = 128
        REL_DIM = 128
        in_fts = context @ W_common.T
        left = in_fts @ w_left + b_left
        right = in_fts @ w_right + b_right
        logits = left[:, None] + right[None, :]
        logits = jnp.where(logits >= 0, logits, 0.2 * logits)
        logits = jnp.where(adj_tensor <= 0.0, -jnp.inf, logits)
        coefs = jax.nn.softmax(logits, axis=-1)
        x = coefs @ relation
        return jax.nn.relu(x)
    h = jnp.maximum(_layernorm(x, axis=-1), 0.0)
    x = x + _L0_gnn_ref(h, adj, L0_gnn_weight, L0_gnn_bias)
    h = jnp.maximum(_layernorm(x, axis=-1), 0.0)
    x = x + _L1_gnn_ref(h, L1_gnn_context, adj, L1_gnn_W_common, L1_gnn_w_left, L1_gnn_b_left, L1_gnn_w_right, L1_gnn_b_right)
    return x

_drawn_inputs = setup_inputs


def setup_inputs(seed=0):
    import zlib

    import numpy as np

    out = dict(_drawn_inputs(seed))
    spreads = {}
    factors = {}
    for name, (base, spread) in spreads.items():
        noise = np.random.default_rng([zlib.crc32(name.encode()), seed]).standard_normal(out[name].shape)
        drawn = base * np.exp(spread * noise) if base else spread * noise
        out[name] = jnp.asarray(drawn.astype(out[name].dtype))
    for name, factor in factors.items():
        out[name] = (out[name] * factor).astype(out[name].dtype)
    return out
```

```python
from contextlib import ExitStack

import concourse.bass as bass
from concourse import mybir

F32 = mybir.dt.float32
F16 = mybir.dt.float16
BF16 = mybir.dt.bfloat16
I8 = mybir.dt.int8
ALU = mybir.AluOpType
ACT = mybir.ActivationFunctionType
AX_X = mybir.AxisListType.X
RMAX = bass.bass_isa.ReduceOp.max

P = 128
Q = 32
NQ = P // Q
L = 4
CH = L * P
XSLOTS = 4
HB = 2
HALVES = L // HB

MIN_NORM2 = 1e-30
MAX_NORM = 1.0 - 1e-5
ARTANH_RIM = 6.103033822758835
ARTANH_CLIP = 1.0 - 1e-7
LN_EPS = 1e-5
SLOPE = 0.2
SCALE = 4096.0


class Steps:

    def __init__(self, eng, sem, base=0):
        self.eng, self.sem, self.base, self.n = eng, sem, base, 0

    def __call__(self, ins):
        self.n += 1
        ins.then_inc(self.sem, 1)
        self.eng.wait_ge(self.sem, self.base + self.n)


def bass_two_graph_layers(nc, x, adj, weight, bias, context, w_common, w_left, b_left, w_right, b_right, out):
    N, D = x.shape
    C = context.shape[1]
    NK = N // P
    NC = N // CH
    TH = NC * HALVES
    GW = 2 * D + 2
    assert D == P and NC % 2 == 0 and NC >= 4 and w_common.shape == (P, C)

    with ExitStack() as ctx:
        def sb(name, shape, dt):
            return ctx.enter_context(nc.sbuf_tensor(name, shape, dt))

        def sem(name):
            return ctx.enter_context(nc.semaphore(name))

        mask = sb("mask", [P, NC, NK, CH], I8)
        h2_room = sb("h2_room", [P, NK * D * 4], I8)
        room = sb("room", [P, NK * D * 4 + XSLOTS * CH * L * 4 + 2 * HB * CH * 4], I8)
        support_T = sb("support_T", [P, CH], F32)
        relu_u = sb("relu_u", [P, L, D], F32)
        xk = sb("xk", [P, L, D], F32)
        ident = sb("ident", [P, P], F32)
        l_col = sb("l_col", [P, NK], F32)
        r_col = sb("r_col", [P, NK], F32)
        a_col = sb("a_col", [P, NK], F32)
        b_col = sb("b_col", [P, NK], F32)
        s1_col = sb("s1_col", [P, NK], F32)
        s0_col = sb("s0_col", [P, NK], F32)
        post = sb("post", [P, 64], F32)
        stats = sb("stats", [P, L, 6], F32)
        mv = sb("mv", [P, L, 2], F32)

        def view(tensor, offset, shape, dt):
            size = {F32: 4, F16: 2, BF16: 2}[dt]
            n = 1
            for s in shape:
                n *= s
            v = tensor[:, offset:offset + n * size].bitcast(dt)
            if len(shape) == 2:
                v = v.rearrange("p (a b) -> p a b", a=shape[0])
            if len(shape) == 3:
                v = v.rearrange("p (a b c) -> p a b c", a=shape[0], b=shape[1])
            return v

        o = 0
        xt = view(room, o, [NK, D], F32)
        o += NK * D * 4
        loaded = view(room, o, [XSLOTS, L * NQ, L * Q], F32)
        o += XSLOTS * CH * L * 4
        turned = view(room, o, [2, HB, CH], F32)
        o = 0
        G = [None, None]
        for w in (0, 1):
            G[w] = view(room, o, [NK, GW], F16)
            o += NK * GW * 2
        pos = view(room, o, [2, L, CH], BF16)
        o += 2 * L * CH * 2
        neg = view(room, o, [2, L, CH], BF16)
        o += 2 * L * CH * 2
        edge = view(room, o, [2, HB, CH], BF16)
        o += 2 * HB * CH * 2
        nl_even = view(room, o, [CH], F32)
        h2 = view(h2_room, 0, [NK, D], F32)
        o = 0
        nl_odd = view(h2_room, o, [CH], F32)
        o += CH * 4
        summed = view(h2_room, o, [L, GW], F32)
        o += L * GW * 4
        neg_part = view(h2_room, o, [2, GW], F32)
        o += 2 * GW * 4
        y = view(h2_room, o, [L, D], F32)
        o += L * D * 4
        x1k = view(h2_room, o, [L, D], F32)
        nl = [nl_even, nl_odd]

        scratch = mask[:, :, :, :].rearrange("p c k i -> p (c k i)")
        o = 2 * NK * CH
        x_in = view(scratch, o, [NK, D], F32)
        o += NK * D * 4
        spent = view(scratch, o - NK * D * 4, [NK, C], F32)
        h = view(scratch, o, [NK, D], F32)
        o += NK * D * 4
        mx = view(scratch, o, [NK, D], F32)
        o += NK * D * 4
        cx = view(scratch, o, [NK, C], F32)
        o += NK * C * 4
        W_in = view(scratch, o, [D], F32)
        o += D * 4
        WT = view(scratch, o, [D], F32)
        o += D * 4
        WTb = view(scratch, o, [1], F32)
        o += 4
        b_colv = view(scratch, o, [1], F32)
        o += 4
        hb_colv = view(scratch, o, [1], F32)
        o += 4
        bias_b = view(scratch, o, [D], F32)
        o += D * 4
        hb = view(scratch, o, [D], F32)
        o += D * 4
        Wc = view(scratch, o, [C], F32)
        o += C * 4
        wlr = view(scratch, o, [4], F32)
        o += 4 * 4
        wl_b = view(scratch, o, [2, P], F32)
        o += 2 * P * 4
        hT = view(scratch, o, [2, L * P], F32)
        o += 2 * L * P * 4
        junk = view(scratch, o, [L, D], F32)
        o += L * D * 4
        fb = view(scratch, o, [2, D], F32)
        o += 2 * D * 4
        stats0 = view(scratch, o, [NK, 6], F32)
        o += NK * 6 * 4
        mv0 = view(scratch, o, [NK, 2], F32)
        o += NK * 2 * 4
        sv = view(scratch, o, [24, NK], F32)
        o += 24 * NK * 4
        nlT = view(scratch, o, [P], F32)
        o += P * 4
        assert o <= NC * NK * CH

        ps = ctx.enter_context(nc.psum_tensor("ps", [P, 8, 512], F32))
        acc = [ps[:, 0, :], ps[:, 1, :]]
        support = ps[:, 2, :].rearrange("p (l d) -> p l d", l=L)
        sq1 = ps[:, 3, :].rearrange("p (l d) -> p l d", l=L)
        sq2 = ps[:, 4, :].rearrange("p (l d) -> p l d", l=L)
        ps_hT = [ps[:, 2, :], ps[:, 3, :]]
        ps_mx = [ps[:, 4, :].rearrange("p (l d) -> p l d", l=L), ps[:, 5, :].rearrange("p (l d) -> p l d", l=L)]
        ps_mb = ps[:, 6, 0:NK]
        ps_small = ps[:, 7, :]
        ps_v = ps[:, 0, :].rearrange("p (w c) -> p w c", w=2)

        nl_dram = nc.dram_tensor("neg_left", (NK, P), F32, kind="Internal").ap()

        weights_in = sem("weights_in")
        x_in_sem = [sem(f"x_loaded_{s}") for s in range(NC)]
        cx_in = sem("context_loaded")
        zeroed = sem("ident_zeroed")
        ident_made = sem("ident_made")
        adj_in = [sem(f"adj_loaded_{s}") for s in range(XSLOTS)]
        half_turned = sem("half_turned")
        half_multiplied = sem("half_multiplied")
        half_signed = sem("half_signed")
        dve_step = sem("dve_step")
        pool_step = sem("pool_step")
        small_turned = sem("small_turned")
        wt_copied = sem("wt_copied")
        sqrt_asked, sqrt_done = sem("sqrt_asked"), sem("sqrt_done")
        affine_ready = sem("affine_ready")
        h_ready = sem("h_ready")
        hT_turned, hT_copied = sem("hT_turned"), sem("hT_copied")
        mx_done, mx_squared, mx_copied, mx_summed = (sem("mx_done"), sem("mx_squared"), sem("mx_copied"),
                                                     sem("mx_summed"))
        act_asked, act_done = sem("act_asked"), sem("act_done")
        tangent_scales = sem("tangent_scales")
        fb_ready, xt_ready = sem("fb_ready"), sem("xt_ready")
        wl_ready, v_ready = sem("wl_ready"), sem("v_ready")
        rmax_part, rmax_all = sem("rmax_part"), sem("rmax_all")
        nl_ready, nl_turned, nl_copied, nl_stored = (sem("nl_ready"), sem("nl_turned"), sem("nl_copied"),
                                                     sem("nl_stored"))
        expo_asked, expo_done = sem("expo_asked"), sem("expo_done")
        support_copied, support_turned = sem("support_copied"), sem("support_turned")
        relu_ready, u_squared, relu_squared = sem("relu_ready"), sem("u_squared"), sem("relu_squared")
        sums_ready, norms_ready = sem("sums_ready"), sem("norms_ready")
        shrunk_ready, tanh_ready = sem("shrunk_ready"), sem("tanh_ready")
        xk_loaded, x1_ready, x1_stored = sem("xk_loaded"), sem("x1_ready"), sem("x1_stored")
        var_ready, std_ready, norm2_ready, h2_ready = (sem("var_ready"), sem("std_ready"), sem("norm2_ready"),
                                                       sem("h2_ready"))
        nl_loaded = [sem("nl_loaded_even"), sem("nl_loaded_odd")]
        weight_cols = sem("weight_cols")
        head_ready, rest_ready = sem("head_ready"), sem("rest_ready")
        edge_ready, parts_ready, parts_used = sem("edge_ready"), sem("parts_ready"), sem("parts_used")
        rows_summed, neg_scaled, rows_taken = sem("rows_summed"), sem("neg_scaled"), sem("rows_taken")
        recip_ready, summed_read = sem("recip_ready"), sem("summed_read")
        y_relu = sem("y_relu")
        x1_loaded, y_ready, out_stored = sem("x1_loaded"), sem("y_ready"), sem("out_stored")

        def nodes(t):
            return t.rearrange("(s b l q) d -> s b q l d", b=NQ, l=L, q=Q)

        x_n, cx_n, out_n = nodes(x), nodes(context), nodes(out)
        adj_n = adj.rearrange("(s r p) (g b j) -> s g b p r j", r=CH // Q, p=Q, b=NQ, j=L * Q)

        def pick(view_, c):
            if isinstance(c, int):
                return view_[c]
            v = view_[bass.ds(c, 1)]
            names = "abdefg"[:len(v.shape) - 1]
            return v.rearrange(f"z {' '.join(names)} -> (z {names[0]}) {' '.join(names[1:])}")

        def chunked(eng, chunk):
            chunk(0, 0)
            chunk(1, 1)
            with eng.Fori(1, NC // 2) as pair:
                chunk(pair * 2, 0)
                chunk(pair * 2 + 1, 1)

        def cols(t, start, n):
            return t[:, start:start + n] if isinstance(start, int) else t[:, bass.ds(start, n)]

        def nl_count(c, parity):
            if isinstance(c, int):
                return 16 * (c // 2 + 1)
            return c * 8 + (8 if parity else 16)

        def mx_out(act, t):
            act.wait_ge(mx_done, t + 1)
            if t >= 1:
                act.wait_ge(mx_summed, t)
            nc.scalar.activation(junk, ps_mx[t % 2], ACT.Square).then_inc(mx_squared, 1)
            nc.scalar.activation(mx[:, t * L:(t + 1) * L, :], ps_mx[t % 2], ACT.Copy).then_inc(mx_copied, 1)

        block = ctx.enter_context(nc.Block())

        @block.sync
        def _(sp):
            sp.dma_start(W_in, weight).then_inc(weights_in, 16)
            sp.dma_start(b_colv, bias.rearrange("(d a) -> d a", a=1)).then_inc(weights_in, 16)
            sp.dma_start(bias_b, bias.rearrange("(a d) -> a d", a=1).broadcast_to([P, D])).then_inc(weights_in, 16)
            for s in range(NC):
                for b in range(NQ):
                    sp.dma_start(x_in[b * Q:(b + 1) * Q, s * L:(s + 1) * L, :], x_n[s, b]).then_inc(x_in_sem[s], 16)
            sp.dma_start(Wc, w_common).then_inc(weights_in, 16)
            for n, w in enumerate((w_left, w_right)):
                sp.dma_start(wlr[:, n:n + 1], w.rearrange("(d a) -> d a", a=1)).then_inc(weights_in, 16)
            for n, w in enumerate((b_left, b_right)):
                sp.dma_start(wlr[:, 2 + n:3 + n], w.broadcast_to([P, 1])).then_inc(weights_in, 16)

            def store_x1(p):
                sp.wait_ge(x1_ready, p + 1)
                os = pick(out_n, p)
                for b in range(NQ):
                    sp.dma_start(os[b], xk[b * Q:(b + 1) * Q]).then_inc(x1_stored, 16)

            def load_x(p):
                if not (isinstance(p, int) and p == 0):
                    sp.wait_ge(x1_stored, p * (16 * NQ))
                    sp.wait_ge(h2_ready, p)
                xs = pick(x_n, p)
                for b in range(NQ):
                    sp.dma_start(xk[b * Q:(b + 1) * Q], xs[b]).then_inc(xk_loaded, 16)

            def load(c, _):
                rows = pick(adj_n, c)
                for g in range(NC):
                    if not (isinstance(c, int) and c == 0 and g < XSLOTS):
                        sp.wait_ge(half_turned, c * TH + HALVES * (g - XSLOTS + 1))
                    for b in range(NQ):
                        sp.dma_start(loaded[b * Q:(b + 1) * Q, g % XSLOTS], rows[g, b]).then_inc(
                            adj_in[g % XSLOTS], 16)
                    if g == 1 and not (isinstance(c, int) and c < 2):
                        store_x1(c - 2)
                    if g == 3 and not (isinstance(c, int) and c < 1):
                        load_x(c - 1)

            chunked(sp, load)
            store_x1(NC - 2)
            load_x(NC - 1)
            store_x1(NC - 1)

            def neg_left_row(c, parity):
                sp.dma_start(nl[parity], (nl_dram[c * L:(c + 1) * L] if isinstance(c, int) else
                                          nl_dram[bass.ds(c * L, L)]).rearrange("(a l) p -> a (l p)", a=1)
                             .broadcast_to([P, CH])).then_inc(nl_loaded[parity], 16)

            def rows_out(p):
                os = pick(out_n, p)
                for b in range(NQ):
                    sp.dma_start(x1k[b * Q:(b + 1) * Q], os[b]).then_inc(x1_loaded, 16)
                sp.wait_ge(y_ready, p + 1)
                for b in range(NQ):
                    sp.dma_start(os[b], y[b * Q:(b + 1) * Q]).then_inc(out_stored, 16)

            def chunk_of_phase_2(c, parity):
                sp.wait_ge(parts_ready, c * TH - TH)
                neg_left_row(c, parity)
                rows_out(c - 2)

            sp.wait_ge(nl_stored, 16)
            sp.wait_ge(half_multiplied, NC * TH)
            sp.wait_ge(half_signed, NC * TH)
            neg_left_row(0, 0)
            sp.wait_ge(x1_stored, NC * 16 * NQ)
            sp.wait_ge(rest_ready, NK)
            neg_left_row(1, 1)
            with sp.Fori(1, NC // 2) as pair:
                chunk_of_phase_2(pair * 2, 0)
                chunk_of_phase_2(pair * 2 + 1, 1)
            rows_out(NC - 2)
            rows_out(NC - 1)
            sp.wait_ge(out_stored, NC * 16 * NQ)

        @block.gpsimd
        def _(pool):
            nc.gpsimd.memset(ident[:], 0.0).then_inc(zeroed, 1)
            pool.wait_ge(zeroed, 1)
            nc.gpsimd.affine_select(out=ident[:], in_=ident[:], compare_op=ALU.not_equal, fill=1.0, base=0,
                                    pattern=[[-1, P]], channel_multiplier=1).then_inc(ident_made, 1)
            for s in range(NC):
                for b in range(NQ):
                    pool.dma_start(cx[b * Q:(b + 1) * Q, s * L:(s + 1) * L, :], cx_n[s, b]).then_inc(cx_in, 16)
            pool.wait_ge(rmax_part, 1)
            nc.gpsimd.partition_all_reduce(post[:, 63:64], post[:, 62:63], P, RMAX).then_inc(rmax_all, 1)
            pool.wait_ge(nl_copied, 1)
            pool.dma_start(nl_dram, nlT[0:NK, :]).then_inc(nl_stored, 16)

            def last_steps(c, parity):
                step = Steps(pool, pool_step, c)
                pool.wait_ge(recip_ready, c + 1)
                if not (isinstance(c, int) and c == 0):
                    pool.wait_ge(out_stored, c * (16 * NQ))
                step(nc.gpsimd.tensor_tensor(y, summed[:, :, 0:D], summed[:, :, D:2 * D], ALU.add))
                ins = nc.gpsimd.tensor_tensor(y, y, post[:, 52:52 + L].unsqueeze(2).broadcast_to([P, L, D]), ALU.mult)
                ins.then_inc(summed_read, 1)
                pool.wait_ge(y_relu, c + 1)
                pool.wait_ge(x1_loaded, c * (16 * NQ) + 16 * NQ)
                nc.gpsimd.tensor_tensor(y, y, x1k, ALU.add).then_inc(y_ready, 1)
            chunked(pool, last_steps)

        @block.tensor
        def _(pe):
            pe.wait_ge(ident_made, 1)
            pe.wait_ge(weights_in, 16 * 8)
            pe.transpose(ps_small[:, 0:P], W_in, ident[:]).then_inc(small_turned, 1)
            pe.wait_ge(wt_copied, 1)
            pe.matmul(ps_small[:, P:P + 1], W_in, hb_colv, start=True, stop=True).then_inc(small_turned, 1)
            pe.wait_ge(wl_ready, 1)
            pe.matmul(ps_v[:, 0, :], wl_b[:, 0, :], Wc, start=True, stop=True)
            pe.matmul(ps_v[:, 1, :], wl_b[:, 1, :], Wc, start=True, stop=True).then_inc(v_ready, 1)
            pe.wait_ge(wt_copied, 2)
            for s in range(NC + 1):
                if s < NC:
                    pe.wait_ge(h_ready, L * (s + 1))
                    if s >= 2:
                        pe.wait_ge(hT_copied, s - 1)
                    for l in range(L):
                        mm = pe.transpose(ps_hT[s % 2][:, l * P:(l + 1) * P], h[:, s * L + l, :], ident[:])
                    mm.then_inc(hT_turned, 1)
                if s >= 1:
                    t = s - 1
                    pe.wait_ge(hT_copied, t + 1)
                    if t >= 2:
                        pe.wait_ge(mx_squared, t - 1)
                        pe.wait_ge(mx_copied, t - 1)
                    for l in range(L):
                        lhs = hT[:, t % 2, l * P:(l + 1) * P]
                        pe.matmul(ps_mx[t % 2][:, l, :], lhs, WT, start=True, stop=True)
                        mm = pe.matmul(ps_mb[:, t * L + l:t * L + l + 1], lhs, WTb, start=True, stop=True)
                    mm.then_inc(mx_done, 1)
            pe.wait_ge(nl_ready, 1)
            pe.transpose(ps_small[0:NK, 256:256 + P], sv[:, 23, :], ident[:]).then_inc(nl_turned, 1)

            def turn_support(p):
                pe.wait_ge(support_copied, p + 1)
                if not (isinstance(p, int) and p == 0):
                    pe.wait_ge(relu_ready, p)
                    pe.wait_ge(u_squared, p)
                else:
                    pe.wait_ge(xt_ready, NK)
                for l in range(L):
                    mm = pe.transpose(support[:, l, :], support_T[:, l * P:(l + 1) * P], ident[:])
                mm.then_inc(support_turned, 1)

            def product(c, parity):
                number = isinstance(c, int)
                if not number or c >= 2:
                    pe.wait_ge(support_copied, c - 1)
                for g in range(NC):
                    for hf in range(HALVES):
                        half = g * HALVES + hf
                        pe.wait_ge(half_turned, c * TH + half + 1)
                        for kk in range(HB):
                            k = g * L + hf * HB + kk
                            if number and c == 0:
                                pe.wait_ge(xt_ready, k + 1)
                            mm = pe.matmul(acc[parity], xt[:, k, :], turned[:, half % 2, kk, :],
                                           start=(k == 0), stop=(k == NK - 1))
                        mm.then_inc(half_multiplied, 1)
                        if half == 2 and not (number and c == 0):
                            turn_support(c - 1)
            chunked(pe, product)
            turn_support(NC - 1)

            def attend(c, parity):
                number = isinstance(c, int)
                for g in range(NC):
                    pe.wait_ge(parts_ready, c * TH + HALVES * (g + 1))
                    for t in range(L):
                        if g == 0 and not (number and c == 0):
                            pe.wait_ge(rows_taken, c * L + t - L + 1)
                        if g == 0 and t == 0 and number and c == 0:
                            pe.wait_ge(sums_ready, NC)
                            pe.wait_ge(weight_cols, 1)
                        for kk in range(L):
                            k = g * L + kk
                            if number and c == 0 and t == 0:
                                pe.wait_ge(head_ready, 2 * (k + 1))
                                pe.wait_ge(rest_ready, k + 1)
                            for w, part in ((0, neg), (1, pos)):
                                mm = pe.matmul(ps[:, 2 * t + w, 0:GW], part[:, g % 2, kk, t * P:(t + 1) * P],
                                               G[w][:, k, :], start=(k == 0), stop=(k == NK - 1))
                        if g == NC - 1:
                            mm.then_inc(rows_summed, 1)
                        elif t == L - 1:
                            mm.then_inc(parts_used, 1)
            chunked(pe, attend)

        @block.scalar
        def _(act):
            act.wait_ge(sqrt_asked, 1)
            nc.scalar.activation(post[:, 1:2], post[:, 0:1], ACT.Sqrt).then_inc(sqrt_done, 1)
            act.wait_ge(sqrt_asked, 2)
            nc.scalar.activation(sv[:, 1, :], sv[:, 0, :], ACT.Sqrt).then_inc(sqrt_done, 1)
            act.wait_ge(sqrt_done, 1)
            nc.scalar.activation(post[:, 2:3], post[:, 1:2], ACT.Tanh).then_inc(sqrt_done, 1)
            act.wait_ge(affine_ready, 1)
            for k in range(NK):
                nc.scalar.activation(h[:, k, :], x_in[:, k, :], ACT.Relu, bias=sv[:, 3, k:k + 1],
                                     scale=sv[:, 2, k:k + 1]).then_inc(h_ready, 1)
                if k % L == L - 1 and k >= 2 * L:
                    mx_out(act, k // L - 2)
            mx_out(act, NC - 2)
            mx_out(act, NC - 1)
            act.wait_ge(act_asked, 1)
            nc.scalar.activation(sv[:, 5:7, :], sv[:, 5:7, :], ACT.Sqrt).then_inc(act_done, 1)
            act.wait_ge(act_asked, 2)
            nc.scalar.activation(sv[:, 8:10, :], sv[:, 8:10, :], ACT.Ln).then_inc(act_done, 1)
            act.wait_ge(act_asked, 3)
            nc.scalar.activation(sv[:, 11, :], sv[:, 11, :], ACT.Tanh).then_inc(act_done, 1)
            act.wait_ge(act_asked, 4)
            nc.scalar.activation(sv[:, 5, :], sv[:, 5, :], ACT.Sqrt).then_inc(act_done, 1)
            act.wait_ge(act_asked, 5)
            nc.scalar.activation(sv[:, 8:10, :], sv[:, 8:10, :], ACT.Ln).then_inc(act_done, 1)
            act.wait_ge(tangent_scales, 1)
            for k in range(NK):
                if k >= 2:
                    act.wait_ge(xt_ready, k - 1)
                nc.scalar.activation(fb[:, k % 2, :], hb, ACT.Copy, scale=sv[:, 14, k:k + 1]).then_inc(fb_ready, 1)
            act.wait_ge(expo_asked, 1)
            nc.scalar.activation(sv[:, 16:20, :], sv[:, 16:20, :], ACT.Exp).then_inc(expo_done, 1)

            def post_steps(p):
                row = p * L

                def copy():
                    act.wait_ge(half_multiplied, p * TH + TH)
                    if not (isinstance(p, int) and p == 0):
                        act.wait_ge(support_turned, p)
                    nc.scalar.activation(support_T[:], acc_of[0], ACT.Copy).then_inc(support_copied, 1)

                def squares():
                    act.wait_ge(relu_ready, p + 1)
                    nc.scalar.activation(sq1, support, ACT.Square).then_inc(u_squared, 1)
                    nc.scalar.activation(sq2, relu_u[:], ACT.Square).then_inc(relu_squared, 1)

                def norms():
                    act.wait_ge(sums_ready, p + 1)
                    nc.scalar.activation(post[:, 8:16], post[:, 0:8], ACT.Sqrt).then_inc(norms_ready, 1)

                def tanh():
                    act.wait_ge(shrunk_ready, p + 1)
                    nc.scalar.activation(post[:, 28:32], post[:, 24:28], ACT.Tanh).then_inc(tanh_ready, 1)

                def std():
                    act.wait_ge(var_ready, p + 1)
                    nc.scalar.activation(post[:, 44:48], post[:, 40:44], ACT.Sqrt).then_inc(std_ready, 1)

                def normed():
                    act.wait_ge(norm2_ready, p + 1)
                    for l in range(L):
                        dst = (h2[:, row + l, :] if isinstance(p, int) else
                               h2[:, bass.ds(row + l, 1), :].rearrange("p o d -> p (o d)"))
                        ins = nc.scalar.activation(dst, xk[:, l, :], ACT.Relu, bias=post[:, 36 + l:37 + l],
                                                   scale=post[:, 48 + l:49 + l])
                    ins.then_inc(h2_ready, 1)
                return {0: copy, 4: squares, 6: norms, 8: tanh, 10: std, 12: normed}

            acc_of = [None]

            def signs(c, parity):
                number = isinstance(c, int)
                acc_of[0] = acc[1 - parity]
                steps = {} if number and c == 0 else post_steps(c - 1)
                mc = mask[:, c] if number else mask[:, bass.ds(c, 1)].rearrange("p o k i -> p (o k) i")
                if number and c == 1:
                    act.wait_ge(nl_stored, 16)
                for half in range(TH):
                    act.wait_ge(half_turned, c * TH + half + 1)
                    nc.scalar.activation(mc[:, half * HB:(half + 1) * HB, :], turned[:, half % 2], ACT.Sign).then_inc(
                        half_signed, 1)
                    if half in steps:
                        steps[half]()
            chunked(act, signs)
            acc_of[0] = acc[1]
            steps = post_steps(NC - 1)
            for name in sorted(steps):
                steps[name]()

            def edges(c, parity):
                number = isinstance(c, int)
                mc = mask[:, c] if number else mask[:, bass.ds(c, 1)].rearrange("p o k i -> p (o k) i")
                for g in range(NC):
                    if number and c == 0:
                        act.wait_ge(h2_ready, NC)
                        for k in range(g * L, g * L + L):
                            for w, s_col in ((0, s0_col), (1, s1_col)):
                                nc.scalar.activation(G[w][:, k, 0:D], h2[:, k, :], ACT.Copy,
                                                     scale=s_col[:, k:k + 1]).then_inc(head_ready, 1)
                    for hf in range(HALVES):
                        half = g * HALVES + hf
                        if not (number and c == 0 and half < 2):
                            act.wait_ge(parts_ready, c * TH + half - 1)
                        nc.scalar.activation(edge[:, half % 2], mc[:, half * HB:(half + 1) * HB, :],
                                             ACT.Relu).then_inc(edge_ready, 1)
                    if g == 0 and not (number and c == 0):
                        scale_rows(c - 1)
                    if g == NC // 2 and not (number and c == 0):
                        relu_rows(c - 1)

            def relu_rows(p):
                act.wait_ge(summed_read, p + 1)
                nc.scalar.activation(y, y, ACT.Relu).then_inc(y_relu, 1)

            def scale_rows(p):
                for t in range(L):
                    act.wait_ge(rows_summed, p * L + t + 1)
                    if not (isinstance(p, int) and p == 0 and t < 2):
                        act.wait_ge(rows_taken, p * L + t - 1)
                    nc.scalar.activation(neg_part[:, t % 2, :], ps[:, 2 * t, 0:GW], ACT.Copy,
                                         scale=cols(b_col, p * L + t, 1)).then_inc(neg_scaled, 1)
            chunked(act, edges)
            scale_rows(NC - 1)
            relu_rows(NC - 1)

        @block.vector
        def _(dve):
            v = nc.vector
            step = Steps(dve, dve_step)

            dve.wait_ge(weights_in, 16 * 8)
            step(v.tensor_tensor(hb, bias_b, bias_b, ALU.mult))
            step(v.reduce_sum(post[:, 0:1], hb, AX_X))
            v.tensor_scalar(post[:, 0:1], post[:, 0:1], MIN_NORM2, None, ALU.max).then_inc(sqrt_asked, 1)
            step(v.memset(junk[:, 0, :], 1.0))
            v.tensor_scalar(wl_b[:, 0, :], junk[:, 0, :], wlr[:, 0:1], None, ALU.mult)
            v.tensor_scalar(wl_b[:, 1, :], junk[:, 0, :], wlr[:, 1:2], None, ALU.mult).then_inc(wl_ready, 1)
            for s in range(NC):
                dve.wait_ge(x_in_sem[s], 16 * NQ)
                for k in range(s * L, s * L + L):
                    ins = v.bn_stats(stats0[:, k, :], x_in[:, k, :])
            step(ins)
            for k in range(NK):
                ins = v.bn_aggr(mv0[:, k, :], stats0[:, k, :])
            step(ins)
            dve.wait_ge(sqrt_done, 1)
            v.tensor_scalar(sv[:, 0, :], mv0[:, :, 1], LN_EPS, None, ALU.add).then_inc(sqrt_asked, 1)
            dve.wait_ge(small_turned, 1)
            v.tensor_copy(WT, ps_small[:, 0:P])
            dve.wait_ge(sqrt_done, 3)
            step(v.reciprocal(sv[:, 2, :], sv[:, 1, :]))
            v.scalar_tensor_tensor(out=sv[:, 3, :], in0=mv0[:, :, 0], scalar=-1.0, in1=sv[:, 2, :], op0=ALU.mult,
                                   op1=ALU.mult).then_inc(affine_ready, 1)
            step(v.reciprocal(post[:, 3:4], post[:, 1:2]))
            step(v.scalar_tensor_tensor(out=post[:, 4:5], in0=post[:, 2:3], scalar=MAX_NORM, in1=post[:, 3:4],
                                        op0=ALU.min, op1=ALU.mult))
            v.tensor_scalar(hb_colv, b_colv, post[:, 4:5], None, ALU.mult).then_inc(wt_copied, 1)
            step(v.tensor_scalar(hb, bias_b, post[:, 4:5], None, ALU.mult))
            step(v.tensor_tensor(junk[:, 1, :], hb, hb, ALU.mult))
            step(v.reduce_sum(post[:, 5:6], junk[:, 1, :], AX_X))
            b2 = post[:, 5:6]
            dve.wait_ge(small_turned, 2)
            v.tensor_copy(WTb, ps_small[:, P:P + 1]).then_inc(wt_copied, 1)

            for s in range(NC + 1):
                if s < NC:
                    dve.wait_ge(hT_turned, s + 1)
                    if s >= 2:
                        dve.wait_ge(mx_done, s - 1)
                    v.tensor_copy(hT[:, s % 2, :], ps_hT[s % 2]).then_inc(hT_copied, 1)
                    hs = h[:, s * L:(s + 1) * L, :]
                    step(v.tensor_tensor(x_in[:, s * L:(s + 1) * L, :], hs, hs, ALU.mult))
                    v.reduce_sum(sv[:, 5, s * L:(s + 1) * L], x_in[:, s * L:(s + 1) * L, :], AX_X)
                if s >= 1:
                    t = s - 1
                    dve.wait_ge(mx_squared, t + 1)
                    v.reduce_sum(sv[:, 6, t * L:(t + 1) * L], junk, AX_X).then_inc(mx_summed, 1)
            step(v.tensor_copy(sv[:, 7, :], ps_mb))

            HN, MN, MB, P1, X2, T1, T2 = (sv[:, n, :] for n in (5, 6, 7, 10, 12, 13, 14))
            def artanh_over(n, dst, cap, asked):
                lo, hi = sv[:, 8, :], sv[:, 9, :]
                p, q, s, m = sv[:, 15, :], sv[:, 20, :], sv[:, 21, :], sv[:, 22, :]
                step(v.tensor_scalar(p, n, cap, None, ALU.min))
                v.tensor_scalar(lo, p, 1.0, None, ALU.add)
                v.tensor_scalar(hi, p, -1.0, 1.0, ALU.mult, ALU.add).then_inc(act_asked, 1)
                step(v.tensor_tensor(q, p, p, ALU.mult))
                step(v.tensor_scalar(s, q, 1.0 / 13, 1.0 / 11, ALU.mult, ALU.add))
                for c in (1 / 9, 1 / 7, 1 / 5, 1 / 3, 1.0):
                    step(v.tensor_tensor(s, s, q, ALU.mult))
                    step(v.tensor_scalar(s, s, c, None, ALU.add))
                step(v.tensor_tensor(s, s, p, ALU.mult))
                step(v.tensor_scalar(m, p, 0.3, None, ALU.is_lt))
                dve.wait_ge(act_done, asked)
                step(v.tensor_tensor(lo, lo, hi, ALU.subtract))
                step(v.tensor_scalar(lo, lo, 0.5, None, ALU.mult))
                step(v.tensor_tensor(s, s, lo, ALU.subtract))
                step(v.tensor_tensor(s, s, m, ALU.mult))
                step(v.tensor_tensor(lo, lo, s, ALU.add))
                step(v.reciprocal(q, n))
                step(v.tensor_tensor(dst, lo, q, ALU.mult))

            v.tensor_scalar(sv[:, 5:7, :], sv[:, 5:7, :], MIN_NORM2, None, ALU.max).then_inc(act_asked, 1)
            dve.wait_ge(act_done, 1)
            artanh_over(HN, T1, ARTANH_CLIP, 2)
            v.tensor_tensor(sv[:, 11, :], T1, MN, ALU.mult).then_inc(act_asked, 1)
            dve.wait_ge(act_done, 3)
            step(v.tensor_scalar(P1, sv[:, 11, :], MAX_NORM, None, ALU.min))
            step(v.tensor_tensor(X2, P1, P1, ALU.mult))
            step(v.reciprocal(T1, MN))
            step(v.tensor_tensor(P1, P1, T1, ALU.mult))
            XY = sv[:, 16, :]
            step(v.tensor_tensor(XY, P1, MB, ALU.mult))
            step(v.tensor_scalar(XY, XY, 2.0, 1.0, ALU.mult, ALU.add))
            A, B, DEN = sv[:, 17, :], sv[:, 18, :], sv[:, 19, :]
            v.tensor_scalar(A, XY, b2, None, ALU.add)
            v.tensor_scalar(B, X2, -1.0, 1.0, ALU.mult, ALU.add)
            step(v.scalar_tensor_tensor(out=DEN, in0=X2, scalar=b2, in1=XY, op0=ALU.mult, op1=ALU.add))
            step(v.tensor_scalar(DEN, DEN, 1e-15, None, ALU.max))
            step(v.reciprocal(DEN, DEN))
            v.tensor_tensor(B, B, DEN, ALU.mult)
            step(v.tensor_tensor(A, A, P1, ALU.mult))
            step(v.tensor_tensor(A, A, DEN, ALU.mult))
            step(v.tensor_tensor(T1, MN, A, ALU.mult))
            step(v.tensor_tensor(T1, T1, T1, ALU.mult))
            step(v.tensor_tensor(T2, A, B, ALU.mult))
            step(v.tensor_tensor(T2, T2, MB, ALU.mult))
            step(v.scalar_tensor_tensor(out=T1, in0=T2, scalar=2.0, in1=T1, op0=ALU.mult, op1=ALU.add))
            step(v.tensor_tensor(T2, B, B, ALU.mult))
            step(v.scalar_tensor_tensor(out=HN, in0=T2, scalar=b2, in1=T1, op0=ALU.mult, op1=ALU.add))
            v.tensor_scalar(HN, HN, MIN_NORM2, None, ALU.max).then_inc(act_asked, 1)
            dve.wait_ge(act_done, 4)
            artanh_over(HN, T1, MAX_NORM, 5)
            v.tensor_tensor(T2, B, T1, ALU.mult)
            v.tensor_tensor(T1, A, T1, ALU.mult).then_inc(tangent_scales, 1)
            dve.wait_ge(tangent_scales, 1)
            for k in range(NK):
                dve.wait_ge(fb_ready, k + 1)
                if k == 0:
                    dve.wait_ge(mx_copied, NC)
                v.scalar_tensor_tensor(out=xt[:, k, :], in0=mx[:, k, :], scalar=T1[:, k:k + 1], in1=fb[:, k % 2, :],
                                       op0=ALU.mult, op1=ALU.add).then_inc(xt_ready, 1)

            dve.wait_ge(cx_in, 16 * NQ * NC)
            dve.wait_ge(v_ready, 1)
            for k in range(NK):
                v.tensor_tensor_reduce(spent[:, k, :], cx[:, k, :], ps_v[:, 0, :], 1.0, 0.0, ALU.mult, ALU.add,
                                       l_col[:, k:k + 1])
                ins = v.tensor_tensor_reduce(cx[:, k, :], cx[:, k, :], ps_v[:, 1, :], 1.0, 0.0, ALU.mult, ALU.add,
                                             r_col[:, k:k + 1])
            step(ins)
            v.tensor_scalar(r_col[:], r_col[:], wlr[:, 3:4], None, ALU.add)
            step(v.tensor_scalar(l_col[:], l_col[:], wlr[:, 2:3], None, ALU.add))
            v.tensor_scalar(sv[:, 23, :], l_col[:], -1.0, None, ALU.mult).then_inc(nl_ready, 1)
            v.reduce_max(post[:, 62:63], r_col[:], AX_X).then_inc(rmax_part, 1)
            dve.wait_ge(nl_turned, 1)
            v.tensor_copy(nlT[0:NK, :], ps_small[0:NK, 256:256 + P]).then_inc(nl_copied, 1)
            dve.wait_ge(rmax_all, 1)
            R = post[:, 63:64]
            E1, E0, EA, EB = (sv[:, n, :] for n in (16, 17, 18, 19))
            v.tensor_scalar(EA, l_col[:], R, None, ALU.add)
            step(v.tensor_scalar(E1, r_col[:], R, None, ALU.subtract))
            v.tensor_scalar(E0, E1, SLOPE, None, ALU.mult)
            step(v.tensor_scalar(EB, EA, SLOPE, None, ALU.mult))
            step(v.tensor_tensor(T1, EA, EB, ALU.max))
            v.tensor_tensor(EA, EA, T1, ALU.subtract)
            v.tensor_tensor(EB, EB, T1, ALU.subtract).then_inc(expo_asked, 1)
            dve.wait_ge(expo_done, 1)
            v.tensor_copy(a_col[:], EA)
            v.tensor_copy(b_col[:], EB)
            v.tensor_scalar(s1_col[:], E1, SCALE, None, ALU.mult)
            step(v.tensor_scalar(s0_col[:], E0, SCALE, None, ALU.mult))
            first_steps = step.n

            POST = 8

            def post_steps(p):
                first = isinstance(p, int) and p == 0
                chain = Steps(dve, dve_step, p * POST + first_steps)
                UN, RN, INV, F, VN, TH_, TF, CO = (post[:, a:b] for a, b in (
                    (8, 12), (12, 16), (16, 20), (20, 24), (24, 28), (28, 32), (32, 36), (56, 60)))

                def relu():
                    dve.wait_ge(support_turned, p + 1)
                    v.tensor_scalar(relu_u[:], support, 0.0, None, ALU.max).then_inc(relu_ready, 1)

                def sums():
                    dve.wait_ge(u_squared, p + 1)
                    v.reduce_sum(post[:, 0:4], sq1, AX_X)
                    dve.wait_ge(relu_squared, p + 1)
                    chain(v.reduce_sum(post[:, 4:8], sq2, AX_X))
                    v.tensor_scalar(post[:, 0:8], post[:, 0:8], MIN_NORM2, None, ALU.max).then_inc(sums_ready, 1)

                def shrink():
                    dve.wait_ge(norms_ready, p + 1)
                    chain(v.reciprocal(INV, UN))
                    chain(v.tensor_scalar(F, INV, ARTANH_RIM, 1.0, ALU.mult, ALU.min))
                    v.tensor_tensor(VN, F, RN, ALU.mult).then_inc(shrunk_ready, 1)

                def residual():
                    dve.wait_ge(tanh_ready, p + 1)
                    v.reciprocal(INV, VN)
                    chain(v.scalar_tensor_tensor(out=TF, in0=TH_, scalar=MAX_NORM, in1=F, op0=ALU.min, op1=ALU.mult))
                    chain(v.tensor_tensor(CO, TF, INV, ALU.mult))
                    dve.wait_ge(xk_loaded, p * (16 * NQ) + 16 * NQ)
                    for l in range(L):
                        ins = v.scalar_tensor_tensor(out=xk[:, l, :], in0=relu_u[:, l, :], scalar=CO[:, l:l + 1],
                                                     in1=xk[:, l, :], op0=ALU.mult, op1=ALU.add)
                    ins.then_inc(x1_ready, 1)
                    dve.wait_ge(x1_ready, p + 1)
                    for l in range(L):
                        ins = v.bn_stats(stats[:, l, :], xk[:, l, :])
                    chain(ins)
                    v.memset(post[:, 61:62], 0.0)
                    for l in range(L):
                        ins = v.bn_aggr(mv[:, l, :], stats[:, l, :])
                    chain(ins)
                    v.tensor_scalar(post[:, 40:44], mv[:, :, 1], LN_EPS, None, ALU.add).then_inc(var_ready, 1)

                def affine():
                    dve.wait_ge(std_ready, p + 1)
                    if not first:
                        dve.wait_ge(h2_ready, p)
                    chain(v.reciprocal(post[:, 48:52], post[:, 44:48]))
                    v.scalar_tensor_tensor(out=post[:, 36:40], in0=mv[:, :, 0], scalar=-1.0, in1=post[:, 48:52],
                                           op0=ALU.mult, op1=ALU.mult).then_inc(norm2_ready, 1)
                    chain_len[0] = chain.n
                return {3: relu, 5: sums, 7: shrink, 9: residual, 11: affine}

            chain_len = [0]

            def turn(c, parity):
                number = isinstance(c, int)
                steps = {} if number and c == 0 else post_steps(c - 1)
                for half in range(TH):
                    g, hf = half // HALVES, half % HALVES
                    if hf == 0:
                        dve.wait_ge(adj_in[g % XSLOTS], c * (16 * NQ * NC // XSLOTS) + 16 * NQ * (g // XSLOTS + 1))
                    if not (number and c == 0 and half < 2):
                        dve.wait_ge(half_multiplied, c * TH + half - 1)
                        dve.wait_ge(half_signed, c * TH + half - 1)
                    for kk in range(HB):
                        l = hf * HB + kk
                        ins = v.transpose(
                            turned[:, half % 2, kk, :].rearrange("p (l b i) -> p b l i", l=L, b=NQ),
                            loaded[:, g % XSLOTS, :, l * Q:(l + 1) * Q].rearrange("p (b l) q -> p b l q", b=NQ))
                    ins.then_inc(half_turned, 1)
                    if half in steps:
                        steps[half]()
            chunked(dve, turn)
            steps = post_steps(NC - 1)
            for at in sorted(steps):
                steps[at]()
            assert chain_len[0] == POST, chain_len
            base2 = first_steps + NC * POST

            dve.wait_ge(h2_ready, NC)
            dve.wait_ge(half_multiplied, NC * TH)
            for w, s_col in ((0, s0_col), (1, s1_col)):
                v.tensor_copy(G[w][:, :, 2 * D], s_col[:])
            chain = Steps(dve, dve_step, base2)
            chain(v.memset(post[:, 60:61], 0.0))
            for w, s_col in ((0, s0_col), (1, s1_col)):
                ins = v.tensor_tensor(G[w][:, :, 2 * D + 1], s_col[:], G[w][:, :, 2 * D], ALU.subtract)
            ins.then_inc(weight_cols, 1)
            base3 = base2 + 1
            SPLIT = TH + 1

            def split(c, parity):
                number = isinstance(c, int)
                chain = Steps(dve, dve_step, c * SPLIT + base3)
                dve.wait_ge(nl_loaded[parity], nl_count(c, parity))
                for g in range(NC):
                    if number and c == 0:
                        for k in range(g * L, g * L + L):
                            dve.wait_ge(head_ready, 2 * (k + 1))
                            for w, s_col in ((0, s0_col), (1, s1_col)):
                                ins = v.scalar_tensor_tensor(out=G[w][:, k, D:2 * D], in0=h2[:, k, :],
                                                             scalar=s_col[:, k:k + 1], in1=G[w][:, k, 0:D],
                                                             op0=ALU.mult, op1=ALU.subtract)
                            ins.then_inc(rest_ready, 1)
                    for hf in range(HALVES):
                        half = g * HALVES + hf
                        dve.wait_ge(edge_ready, c * TH + half + 1)
                        if hf == 0 and g == 1 and not (number and c == 0):
                            dve.wait_ge(rows_summed, c * L)
                        elif hf == 0 and g != 1 and not (number and c == 0 and g == 0):
                            dve.wait_ge(parts_used, c * (NC - 1) + (g - 1 if g else 0))
                        for kk in range(HB):
                            k = half * HB + kk
                            ins = v.scalar_tensor_tensor(out=pos[:, g % 2, hf * HB + kk, :], in0=nl[parity],
                                                         scalar=r_col[:, k:k + 1], in1=edge[:, half % 2, kk, :],
                                                         op0=ALU.is_le, op1=ALU.mult)
                        chain(ins)
                        v.tensor_tensor(neg[:, g % 2, hf * HB:(hf + 1) * HB, :], edge[:, half % 2],
                                        pos[:, g % 2, hf * HB:(hf + 1) * HB, :], ALU.subtract).then_inc(parts_ready, 1)
                    if g == 0 and not (number and c == 0):
                        take_rows(c - 1, chain)
                if number and c == 0:
                    chain(v.memset(post[:, 60:61], 0.0))

            def take_rows(p, chain):
                if not (isinstance(p, int) and p == 0):
                    dve.wait_ge(summed_read, p)
                for t in range(L):
                    dve.wait_ge(neg_scaled, p * L + t + 1)
                    v.scalar_tensor_tensor(out=summed[:, t, :], in0=ps[:, 2 * t + 1, 0:GW],
                                           scalar=cols(a_col, p * L + t, 1), in1=neg_part[:, t % 2, :],
                                           op0=ALU.mult, op1=ALU.add).then_inc(rows_taken, 1)
                dve.wait_ge(rows_taken, p * L + L)
                chain(v.tensor_tensor(post[:, 56:60], summed[:, :, 2 * D], summed[:, :, 2 * D + 1], ALU.add))
                v.reciprocal(post[:, 52:56], post[:, 56:60]).then_inc(recip_ready, 1)

            chunked(dve, split)
            take_rows(NC - 1, Steps(dve, dve_step, base3 + NC * SPLIT))


_INS = ['x', 'adj', 'L0_gnn_weight', 'L0_gnn_bias', 'L1_gnn_context', 'L1_gnn_W_common', 'L1_gnn_w_left',
        'L1_gnn_b_left', 'L1_gnn_w_right', 'L1_gnn_b_right']
_OUTS = [((4096, 128), 'float32')]


def kernel(**inputs):
    import numpy as _np
    import concourse.bacc as _bacc
    from concourse import mybir as _mybir
    from concourse.bass_utils import run_bass_kernel_spmd as _run

    nc = _bacc.Bacc("TRN2", target_bir_lowering=False, num_devices=1)
    arrays, args = {}, []
    for name in _INS:
        a = _np.ascontiguousarray(inputs[name])
        if a.ndim == 0 or name.endswith(("b_left", "b_right")):
            a = a.reshape(1, 1)
        arrays[f"in_{name}_dram"] = a
        args.append(nc.dram_tensor(f"in_{name}_dram", a.shape, _mybir.dt.from_np(a.dtype), kind="ExternalInput").ap())
    for i, (shape, dtype) in enumerate(_OUTS):
        dt = _mybir.dt.from_np(_np.dtype(dtype))
        args.append(nc.dram_tensor(f"out_{i}_dram", shape, dt, kind="ExternalOutput").ap())
    bass_two_graph_layers(nc, *args)
    r = _run(nc, [arrays], core_ids=[0])
    return r.results[0]["out_0_dram"]
```

```python
from contextlib import ExitStack

import concourse.bass as bass
from concourse import mybir

F32 = mybir.dt.float32
F16 = mybir.dt.float16
BF16 = mybir.dt.bfloat16
I8 = mybir.dt.int8
ALU = mybir.AluOpType
ACT = mybir.ActivationFunctionType
AX_X = mybir.AxisListType.X
RMAX = bass.bass_isa.ReduceOp.max

P = 128
Q = 32
NQ = P // Q
L = 4
CH = L * P
XSLOTS = 4
HB = 2
HALVES = L // HB
TSLOTS = 4

MIN_NORM2 = 1e-30
MAX_NORM = 1.0 - 1e-5
ARTANH_RIM = 6.103033822758835
ARTANH_CLIP = 1.0 - 1e-7
LN_EPS = 1e-5
SLOPE = 0.2
SCALE = 4096.0


class Steps:

    def __init__(self, eng, sem, base=0):
        self.eng, self.sem, self.base, self.n = eng, sem, base, 0

    def __call__(self, ins):
        self.n += 1
        ins.then_inc(self.sem, 1)
        self.eng.wait_ge(self.sem, self.base + self.n)


def bass_two_graph_layers(nc, x, adj, weight, bias, context, w_common, w_left, b_left, w_right, b_right, out):
    N, D = x.shape
    C = context.shape[1]
    NK = N // P
    NC = N // CH
    TH = NC * HALVES
    GW = 2 * D + 2
    assert D == P and NC % 2 == 0 and NC >= 4 and w_common.shape == (P, C)

    with ExitStack() as ctx:
        def sb(name, shape, dt):
            return ctx.enter_context(nc.sbuf_tensor(name, shape, dt))

        def sem(name):
            return ctx.enter_context(nc.semaphore(name))

        mask = sb("mask", [P, NC, NK, CH], I8)
        h2_room = sb("h2_room", [P, NK * D * 4], I8)
        phase_1_bytes = NK * D * 4 + XSLOTS * CH * L * 4 + TSLOTS * CH * 4
        phase_2_bytes = 2 * NK * GW * 2 + 3 * 2 * L * CH * 2
        room = sb("room", [P, max(phase_1_bytes, phase_2_bytes) + CH * 4], I8)
        relu_u = sb("relu_u", [P, L, D], F32)
        xk = sb("xk", [P, L, D], F32)
        ident = sb("ident", [P, P], F32)
        r_col = sb("r_col", [P, NK], F32)
        a_col = sb("a_col", [P, NK], F32)
        b_col = sb("b_col", [P, NK], F32)
        s1_col = sb("s1_col", [P, NK], F32)
        s0_col = sb("s0_col", [P, NK], F32)
        post = sb("post", [P, 64], F32)
        stats = sb("stats", [P, L, 6], F32)
        mv = sb("mv", [P, L, 2], F32)
        powers = sb("powers", [P, 2 * L], F32)

        def view(tensor, offset, shape, dt):
            size = {F32: 4, F16: 2, BF16: 2}[dt]
            n = 1
            for s in shape:
                n *= s
            v = tensor[:, offset:offset + n * size].bitcast(dt)
            if len(shape) == 2:
                v = v.rearrange("p (a b) -> p a b", a=shape[0])
            if len(shape) == 3:
                v = v.rearrange("p (a b c) -> p a b c", a=shape[0], b=shape[1])
            return v

        o = 0
        xt = view(room, o, [NK, D], F32)
        o += NK * D * 4
        loaded = view(room, o, [XSLOTS, L * NQ, L * Q], F32)
        o += XSLOTS * CH * L * 4
        turned = view(room, o, [TSLOTS, CH], F32)
        o = room.shape[1] - CH * 4
        support_T = view(room, o, [CH], F32)
        o = 0
        G = [None, None]
        for w in (0, 1):
            G[w] = view(room, o, [NK, GW], F16)
            o += NK * GW * 2
        pos, neg = [], []
        for slots in (pos, neg):
            for _ in range(3):
                slots.append(view(room, o, [L, CH], BF16))
                o += L * CH * 2
        nl_even = support_T
        h2 = view(h2_room, 0, [NK, D], F32)
        o = 0
        nl_odd = view(h2_room, o, [CH], F32)
        o += CH * 4
        summed = view(h2_room, o, [L, GW], F32)
        o += L * GW * 4
        neg_part = view(h2_room, o, [2, GW], F32)
        o += 2 * GW * 4
        y = view(h2_room, o, [L, D], F32)
        o += L * D * 4
        x1k = view(h2_room, o, [L, D], F32)
        nl = [nl_even, nl_odd]

        scratch = mask[:, :, :, :].rearrange("p c k i -> p (c k i)")
        place = [NK * CH]
        for n, slots in enumerate((pos, neg, pos, neg)):
            slots.append(view(scratch, n * L * CH * 2, [L, CH], BF16))

        def tmp(shape):
            n = 4
            for d in shape:
                n *= d
            place[0] += n
            assert place[0] <= NC * NK * CH
            return view(scratch, place[0] - n, shape, F32)

        x_in, h, mx, cx = tmp([NK, D]), tmp([NK, D]), tmp([NK, D]), tmp([NK, C])
        W_in, WT, WTb, b_colv, hb_colv = tmp([D]), tmp([D]), tmp([1]), tmp([1]), tmp([1])
        bias_b, hb, b_sq = tmp([D]), tmp([D]), tmp([D])
        Wc, wlr, vc = tmp([C]), tmp([4]), tmp([2, 2])
        hT, cxT, fb = tmp([2, L * P]), tmp([2, L * P]), tmp([2, D])
        stats0, mv0 = tmp([NK, 6]), tmp([NK, 2])
        sv = tmp([26, NK])
        nlT, l_col = tmp([P]), tmp([NK])

        ps = ctx.enter_context(nc.psum_tensor("ps", [P, 8, 512], F32))
        acc = [ps[:, 0, :], ps[:, 1, :]]
        support, sq1, sq2 = (ps[:, n, :].rearrange("p (l d) -> p l d", l=L) for n in (5, 6, 7))
        ps_hT = [ps[:, 0, :], ps[:, 1, :]]
        ps_mx = [ps[:, n, :].rearrange("p (l d) -> p l d", l=L) for n in (2, 3)]
        ps_mb = ps[:, 4, 0:NK]
        ps_W, ps_v = ps[:, 5, 0:P + 1], ps[:, 5, P + 4:P + 8]
        ps_lr = ps[:, 5, 256:256 + 2 * NK]
        ps_cxT = [ps[:, 6, :], ps[:, 7, :]]
        ps_nl = ps[:, 4, 128:128 + P]

        nl_dram = nc.dram_tensor("neg_left", (NK, P), F32, kind="Internal").ap()

        weights_in, context_weights_in = sem("weights_in"), sem("context_weights_in")
        x_in_sem, cx_in = [sem(f"x_loaded_{l}") for l in range(L)], [sem(f"context_loaded_{l}") for l in range(L)]
        zeroed, ident_made, powers_made = sem("ident_zeroed"), sem("ident_made"), sem("powers_made")
        adj_in = [sem(f"adj_loaded_{s}") for s in range(XSLOTS)]
        block_turned, block_multiplied, half_signed = sem("block_turned"), sem("block_multiplied"), sem("half_signed")
        dve_step, pool_step, weight_heads, weights_summed = (sem("dve_step"), sem("pool_step"), sem("weight_heads"),
                                                            sem("weights_summed"))
        bias_summed, bias_powers, bias_tanh, bias_ready = (sem("bias_summed"), sem("bias_powers"), sem("bias_tanh"),
                                                           sem("bias_ready"))
        small_turned, wt_copied, wtb_made = sem("small_turned"), sem("wt_copied"), sem("wtb_made")
        var0_ready, rstd0_ready, affine_ready, h_ready = (sem("var0_ready"), sem("rstd0_ready"), sem("affine_ready"),
                                                          sem("h_ready"))
        hT_turned, hT_copied, h_squared = sem("hT_turned"), sem("hT_copied"), sem("h_squared")
        mx_done, mx_squared, mx_copied = sem("mx_done"), sem("mx_squared"), sem("mx_copied")
        roots_asked, roots_done = sem("roots_asked"), sem("roots_done")
        act_asked, act_done = sem("act_asked"), sem("act_done")
        tangent_scales, fb_ready, xt_ready = sem("tangent_scales"), sem("fb_ready"), sem("xt_ready")
        v_made, v_copied = sem("v_made"), sem("v_copied")
        cx_turned, cx_copied, lr_made = sem("context_turned"), sem("context_copied"), sem("lr_made")
        rmax_part, rmax_all = sem("rmax_part"), sem("rmax_all")
        nl_ready, nl_turned, nl_copied, nl_stored = (sem("nl_ready"), sem("nl_turned"), sem("nl_copied"),
                                                     sem("nl_stored"))
        expo_asked, expo_done = sem("expo_asked"), sem("expo_done")
        support_copied, support_turned = sem("support_copied"), sem("support_turned")
        relu_ready, u_squared, relu_squared = sem("relu_ready"), sem("u_squared"), sem("relu_squared")
        sums_ready, norms_ready = sem("sums_ready"), sem("norms_ready")
        shrunk_ready, tanh_ready = sem("shrunk_ready"), sem("tanh_ready")
        xk_loaded, x1_ready, x1_stored = sem("xk_loaded"), sem("x1_ready"), sem("x1_stored")
        var_ready, std_ready, norm2_ready, h2_ready = (sem("var_ready"), sem("std_ready"), sem("norm2_ready"),
                                                       sem("h2_ready"))
        nl_loaded = [sem("nl_loaded_even"), sem("nl_loaded_odd")]
        weight_cols = sem("weight_cols")
        head_ready, rest_ready, rest0_ready = sem("head_ready"), sem("rest_ready"), sem("rest0_ready")
        edges_ready, signs_ready, compared, coded = (sem("edges_ready"), sem("signs_ready"), sem("compared"),
                                                     sem("coded"))
        parts_ready, parts_used = sem("parts_ready"), sem("parts_used")
        rows_summed, neg_scaled, rows_taken = sem("rows_summed"), sem("neg_scaled"), sem("rows_taken")
        recip_ready, summed_read = sem("recip_ready"), sem("summed_read")
        y_relu, rest0_scaled, head0_ready = sem("y_relu"), sem("rest0_scaled"), sem("head0_ready")
        x1_loaded, y_ready, out_stored = sem("x1_loaded"), sem("y_ready"), sem("out_stored")

        def nodes(t):
            return t.rearrange("(s b l q) d -> s b q l d", b=NQ, l=L, q=Q)

        x_n, out_n = nodes(x), nodes(out)
        x_l, cx_l = (t.rearrange("(s b l q) d -> l b q s d", b=NQ, l=L, q=Q) for t in (x, context))
        adj_n = adj.rearrange("(s r p) (g b j) -> s g b p r j", r=CH // Q, p=Q, b=NQ, j=L * Q)

        def pick(view_, c):
            if isinstance(c, int):
                return view_[c]
            v = view_[bass.ds(c, 1)]
            names = "abdefg"[:len(v.shape) - 1]
            return v.rearrange(f"z {' '.join(names)} -> (z {names[0]}) {' '.join(names[1:])}")

        def chunked(eng, chunk):
            chunk(0, 0)
            chunk(1, 1)
            with eng.Fori(1, NC // 2) as pair:
                chunk(pair * 2, 0)
                chunk(pair * 2 + 1, 1)

        def cols(t, start, n):
            return t[:, start:start + n] if isinstance(start, int) else t[:, bass.ds(start, n)]

        def nl_count(c, parity):
            if isinstance(c, int):
                return 16 * (c // 2 + 1)
            return c * 8 + (8 if parity else 16)

        def slot(c, g):
            return g % 3 if isinstance(c, int) and c == 0 else (3, 4, 0, 1)[g % 4]

        def by_l(t, l, j=None):
            v = t.rearrange("p (s l) d -> p l s d", l=L)[:, l]
            return v if j is None else v[:, j * L:(j + 1) * L]

        def cols_l(t, l, j=None):
            v = t.rearrange("p (s l) -> p l s", l=L)[:, l]
            return v if j is None else v[:, j * L:(j + 1) * L]

        groups = [(u // 2, u % 2, [L * s + u // 2 for s in range(L * (u % 2), L * (u % 2) + L)])
                  for u in range(NK // L)]
        NG = len(groups)
        assert NK // L // 2 == L

        block = ctx.enter_context(nc.Block())

        @block.sync
        def _(sp):
            for t, src, into in ((x_in, x_l, x_in_sem), (cx, cx_l, cx_in)):
                for l in range(L):
                    for b in range(NQ):
                        sp.dma_start(by_l(t, l)[b * Q:(b + 1) * Q], src[l, b]).then_inc(into[l], 16)

            def store_x1(p):
                sp.wait_ge(x1_ready, p + 1)
                os = pick(out_n, p)
                for b in range(NQ):
                    sp.dma_start(os[b], xk[b * Q:(b + 1) * Q]).then_inc(x1_stored, 16)

            def load_x(p):
                if not (isinstance(p, int) and p == 0):
                    sp.wait_ge(x1_stored, p * (16 * NQ))
                    sp.wait_ge(h2_ready, p)
                xs = pick(x_n, p)
                for b in range(NQ):
                    sp.dma_start(xk[b * Q:(b + 1) * Q], xs[b]).then_inc(xk_loaded, 16)

            def load(c, _):
                rows = pick(adj_n, c)
                for g in range(NC):
                    if not (isinstance(c, int) and c == 0 and g < XSLOTS):
                        sp.wait_ge(block_turned, c * NK + L * (g - XSLOTS + 1))
                    for b in range(NQ):
                        sp.dma_start(loaded[b * Q:(b + 1) * Q, g % XSLOTS], rows[g, b]).then_inc(
                            adj_in[g % XSLOTS], 16)
                    if g == 1 and not (isinstance(c, int) and c < 2):
                        store_x1(c - 2)
                    if g == 3 and not (isinstance(c, int) and c < 1):
                        load_x(c - 1)

            chunked(sp, load)
            store_x1(NC - 2)
            load_x(NC - 1)

            def neg_left_row(c, parity):
                sp.dma_start(nl[parity], (nl_dram[c * L:(c + 1) * L] if isinstance(c, int) else
                                          nl_dram[bass.ds(c * L, L)]).rearrange("(a l) p -> a (l p)", a=1)
                             .broadcast_to([P, CH])).then_inc(nl_loaded[parity], 16)

            def rows_out(p):
                os = pick(out_n, p)
                for b in range(NQ):
                    sp.dma_start(x1k[b * Q:(b + 1) * Q], os[b]).then_inc(x1_loaded, 16)
                sp.wait_ge(y_ready, p + 1)
                for b in range(NQ):
                    sp.dma_start(os[b], y[b * Q:(b + 1) * Q]).then_inc(out_stored, 16)

            def chunk_of_phase_2(c, parity):
                sp.wait_ge(parts_ready, c * NC - NC)
                neg_left_row(c, parity)
                rows_out(c - 2)

            sp.wait_ge(nl_stored, 16)
            sp.wait_ge(block_multiplied, NC * NK)
            sp.wait_ge(half_signed, NC * TH)
            sp.wait_ge(support_turned, NC)
            neg_left_row(0, 0)
            store_x1(NC - 1)
            sp.wait_ge(x1_stored, NC * 16 * NQ)
            sp.wait_ge(rest_ready, NK)
            sp.wait_ge(rest0_ready, NC)
            neg_left_row(1, 1)
            with sp.Fori(1, NC // 2) as pair:
                chunk_of_phase_2(pair * 2, 0)
                chunk_of_phase_2(pair * 2 + 1, 1)
            rows_out(NC - 2)
            rows_out(NC - 1)
            sp.wait_ge(out_stored, NC * 16 * NQ)

        @block.gpsimd
        def _(pool):
            nc.gpsimd.memset(powers[:, 0:L], -0.5)
            nc.gpsimd.memset(powers[:, L:2 * L], 0.5).then_inc(powers_made, 1)
            nc.gpsimd.memset(ident[:], 0.0).then_inc(zeroed, 1)
            pool.wait_ge(zeroed, 1)
            nc.gpsimd.affine_select(out=ident[:], in_=ident[:], compare_op=ALU.not_equal, fill=1.0, base=0,
                                    pattern=[[-1, P]], channel_multiplier=1).then_inc(ident_made, 1)
            pool.dma_start(Wc, w_common).then_inc(context_weights_in, 16)
            for n, w in enumerate((w_left, w_right)):
                pool.dma_start(wlr[:, n:n + 1], w.rearrange("(d a) -> d a", a=1)).then_inc(context_weights_in, 16)
            for n, w in enumerate((b_left, b_right)):
                pool.dma_start(wlr[:, 2 + n:3 + n], w.broadcast_to([P, 1])).then_inc(context_weights_in, 16)
            pool.wait_ge(powers_made, 1)
            inv_root, root = (powers[:, n:n + 1] for n in (0, L))

            def power(dst, src, exponent):
                n = src.shape[1]
                return nc.gpsimd.tensor_tensor(dst, src, exponent.broadcast_to([P, n]), ALU.pow)

            pool.wait_ge(bias_summed, 1)
            power(post[:, 1:2], post[:, 0:1], root)
            power(post[:, 3:4], post[:, 0:1], inv_root).then_inc(bias_powers, 1)
            for l in range(L):
                pool.wait_ge(var0_ready, l + 1)
                power(cols_l(sv[:, 2, :], l), cols_l(sv[:, 0, :], l), inv_root).then_inc(rstd0_ready, 1)
            for u, (l, j, ks) in enumerate(groups):
                pool.wait_ge(h_ready, L * (u + 1))
                nc.gpsimd.tensor_tensor(by_l(x_in, l, j), by_l(h, l, j), by_l(h, l, j), ALU.mult).then_inc(h_squared, 1)
            for n, rows in enumerate((2, 1)):
                pool.wait_ge(roots_asked, n + 1)
                ss = sv[:, 5:5 + rows, :].rearrange("p a k -> p (a k)")
                inv = sv[:, 24:24 + rows, :].rearrange("p a k -> p (a k)")
                power(inv, ss, inv_root).then_inc(roots_done, 1)
                pool.wait_ge(roots_done, 2 * n + 1)
                power(ss, ss, root).then_inc(roots_done, 1)
            pool.wait_ge(rmax_part, 1)
            nc.gpsimd.partition_all_reduce(post[:, 63:64], post[:, 62:63], P, RMAX).then_inc(rmax_all, 1)
            pool.wait_ge(nl_copied, 1)
            pool.dma_start(nl_dram, nlT[0:NK, :]).then_inc(nl_stored, 16)

            def norms(p):
                pool.wait_ge(sums_ready, p + 1)
                nc.gpsimd.tensor_tensor(post[:, 8:16], post[:, 0:8], powers[:], ALU.pow).then_inc(norms_ready, 1)

            def inverse_std(p):
                pool.wait_ge(var_ready, p + 1)
                nc.gpsimd.tensor_tensor(post[:, 48:52], post[:, 40:44], powers[:, 0:L], ALU.pow).then_inc(std_ready, 1)

            with pool.Fori(0, NC - 1) as p:
                norms(p)
                inverse_std(p)
            norms(NC - 1)

            pool.wait_ge(weight_cols, 1)
            for g in range(NC):
                ks, place_of = (slice(n * L, n * L + L) for n in (g, (g - 1) % NC))
                scaled, head, rest = h2[:, place_of, :], G[0][:, ks, 0:D], G[0][:, ks, D:2 * D]
                pool.wait_ge(h2_ready, g + 1)
                if g:
                    pool.wait_ge(rest_ready, g * L)
                nc.gpsimd.tensor_tensor(scaled, h2[:, ks, :], s0_col[:, ks].unsqueeze(2).broadcast_to([P, L, D]),
                                        ALU.mult).then_inc(rest0_scaled, 1)
                pool.wait_ge(rest0_scaled, g + 1)
                nc.gpsimd.tensor_copy(head, scaled).then_inc(head0_ready, 1)
                pool.wait_ge(head0_ready, g + 1)
                nc.gpsimd.tensor_tensor(rest, scaled, head, ALU.subtract).then_inc(rest0_ready, 1)
                if g == 3:
                    inverse_std(NC - 1)

            def last_steps(c, parity):
                step = Steps(pool, pool_step, c)
                pool.wait_ge(recip_ready, c + 1)
                if not (isinstance(c, int) and c == 0):
                    pool.wait_ge(out_stored, c * (16 * NQ))
                step(nc.gpsimd.tensor_tensor(y, summed[:, :, 0:D], summed[:, :, D:2 * D], ALU.add))
                ins = nc.gpsimd.tensor_tensor(y, y, post[:, 52:52 + L].unsqueeze(2).broadcast_to([P, L, D]), ALU.mult)
                ins.then_inc(summed_read, 1)
                pool.wait_ge(y_relu, c + 1)
                pool.wait_ge(x1_loaded, c * (16 * NQ) + 16 * NQ)
                nc.gpsimd.tensor_tensor(y, y, x1k, ALU.add).then_inc(y_ready, 1)
            chunked(pool, last_steps)

        @block.tensor
        def _(pe):
            pe.wait_ge(ident_made, 1)
            pe.wait_ge(weights_in, 16 * 3)
            pe.transpose(ps_W[:, 0:P], W_in, ident[:]).then_inc(small_turned, 1)
            pe.wait_ge(bias_ready, 1)
            pe.matmul(ps_W[:, P:P + 1], W_in, hb_colv, start=True, stop=True).then_inc(small_turned, 1)
            pe.wait_ge(wt_copied, 1)
            pe.wait_ge(wtb_made, 1)
            pe.wait_ge(context_weights_in, 16 * 5)
            for hf in range(2):
                mm = pe.matmul(ps_v[:, 2 * hf:2 * hf + 2], Wc[:, hf * P:(hf + 1) * P], wlr[:, 0:2], start=True,
                               stop=True)
            mm.then_inc(v_made, 1)
            for u in range(NG + 1):
                if u < NG:
                    pe.wait_ge(h_ready, L * (u + 1))
                    if u >= 2:
                        pe.wait_ge(hT_copied, u - 1)
                    for n, k in enumerate(groups[u][2]):
                        mm = pe.transpose(ps_hT[u % 2][:, n * P:(n + 1) * P], h[:, k, :], ident[:])
                    mm.then_inc(hT_turned, 1)
                if u >= 1:
                    t = u - 1
                    pe.wait_ge(hT_copied, t + 1)
                    if t >= 2:
                        pe.wait_ge(mx_copied, t - 1)
                    for n, k in enumerate(groups[t][2]):
                        lhs = hT[:, t % 2, n * P:(n + 1) * P]
                        pe.matmul(ps_mx[t % 2][:, n, :], lhs, WT, start=True, stop=True)
                        mm = pe.matmul(ps_mb[:, k:k + 1], lhs, WTb, start=True, stop=True)
                    mm.then_inc(mx_done, 1)
            pe.wait_ge(v_copied, 1)
            for l in range(L):
                pe.wait_ge(cx_in[l], 16 * NQ)
            for u in range(NK // 2 + 1):
                if u < NK // 2:
                    if u >= 2:
                        pe.wait_ge(cx_copied, u - 1)
                    for n in range(4):
                        mm = pe.transpose(ps_cxT[u % 2][:, n * P:(n + 1) * P],
                                          cx[:, 2 * u + n // 2, (n % 2) * P:(n % 2 + 1) * P], ident[:])
                    mm.then_inc(cx_turned, 1)
                if u >= 1:
                    t = u - 1
                    pe.wait_ge(cx_copied, t + 1)
                    for n in range(4):
                        k = 2 * t + n // 2
                        mm = pe.matmul(ps_lr[:, 2 * k:2 * k + 2], cxT[:, t % 2, n * P:(n + 1) * P],
                                       vc[:, n % 2, :], start=(n % 2 == 0), stop=(n % 2 == 1))
            mm.then_inc(lr_made, 1)

            def turn_support(p):
                pe.wait_ge(support_copied, p + 1)
                if not (isinstance(p, int) and p == 0):
                    pe.wait_ge(relu_ready, p)
                    pe.wait_ge(u_squared, p)
                for l in range(L):
                    mm = pe.transpose(support[:, l, :], support_T[:, l * P:(l + 1) * P], ident[:])
                mm.then_inc(support_turned, 1)

            def product(c, parity):
                number = isinstance(c, int)
                if not number or c >= 2:
                    pe.wait_ge(support_copied, c - 1)
                for k in range(NK):
                    pe.wait_ge(block_turned, c * NK + k + 1)
                    if number and c == 0:
                        pe.wait_ge(xt_ready, k + 1)
                    pe.matmul(acc[parity], xt[:, k, :], turned[:, k % TSLOTS, :],
                              start=(k == 0), stop=(k == NK - 1)).then_inc(block_multiplied, 1)
                    if k == 4 and not (number and c == 0):
                        turn_support(c - 1)
                    if k == 8 and number and c == 0:
                        pe.wait_ge(nl_ready, 1)
                        pe.transpose(ps_nl[0:NK, :], sv[:, 23, :], ident[:]).then_inc(nl_turned, 1)
            chunked(pe, product)
            turn_support(NC - 1)

            def attend(c, parity):
                number = isinstance(c, int)
                for g in range(NC):
                    pe.wait_ge(parts_ready, c * NC + g + 1)
                    for t in range(L):
                        if g == 0 and not (number and c == 0):
                            pe.wait_ge(rows_taken, c * L + t - L + 1)
                        if g == 0 and number and c == 0:
                            if t == 0:
                                pe.wait_ge(weight_cols, 1)
                            if t == 2:
                                pe.wait_ge(sums_ready, NC)
                        for kk in range(L):
                            k = g * L + kk
                            if number and c == 0 and t == 0:
                                pe.wait_ge(rest_ready, k + 1)
                                pe.wait_ge(rest0_ready, g + 1)
                            for w, part in ((0, neg), (1, pos)):
                                mm = pe.matmul(ps[:, 2 * t + w, 0:GW], part[slot(c, g)][:, kk, t * P:(t + 1) * P],
                                               G[w][:, k, :], start=(k == 0), stop=(k == NK - 1))
                        if g == NC - 1:
                            mm.then_inc(rows_summed, 1)
                        elif t == L - 1:
                            mm.then_inc(parts_used, 1)
            chunked(pe, attend)

        @block.scalar
        def _(act):
            act.dma_start(W_in, weight).then_inc(weights_in, 16)
            act.dma_start(b_colv, bias.rearrange("(d a) -> d a", a=1)).then_inc(weights_in, 16)
            act.dma_start(bias_b, bias.rearrange("(a d) -> a d", a=1).broadcast_to([P, D])).then_inc(weights_in, 16)
            act.wait_ge(small_turned, 1)
            nc.scalar.activation(WT, ps_W[:, 0:P], ACT.Copy).then_inc(wt_copied, 1)
            act.wait_ge(bias_powers, 1)
            nc.scalar.activation(post[:, 2:3], post[:, 1:2], ACT.Tanh).then_inc(bias_tanh, 1)

            def copy_hT(u):
                act.wait_ge(hT_turned, u + 1)
                if u >= 2:
                    act.wait_ge(mx_done, u - 1)
                nc.scalar.activation(hT[:, u % 2, :], ps_hT[u % 2], ACT.Copy).then_inc(hT_copied, 1)

            def copy_mx(u):
                l, j, ks = groups[u]
                act.wait_ge(mx_done, u + 1)
                act.wait_ge(h_squared, u + 1)
                nc.scalar.activation(by_l(h, l, j), ps_mx[u % 2], ACT.Square).then_inc(mx_squared, 1)
                nc.scalar.activation(by_l(mx, l, j), ps_mx[u % 2], ACT.Copy).then_inc(mx_copied, 1)

            for u, (l, j, ks) in enumerate(groups):
                act.wait_ge(affine_ready, l + 1)
                for k in ks:
                    nc.scalar.activation(h[:, k, :], x_in[:, k, :], ACT.Relu, bias=sv[:, 3, k:k + 1],
                                         scale=sv[:, 2, k:k + 1]).then_inc(h_ready, 1)
                if u >= 1:
                    copy_hT(u - 1)
                if u >= 2:
                    copy_mx(u - 2)
            copy_hT(NG - 1)
            copy_mx(NG - 2)
            copy_mx(NG - 1)

            def copy_cx(u):
                act.wait_ge(cx_turned, u + 1)
                nc.scalar.activation(cxT[:, u % 2, :], ps_cxT[u % 2], ACT.Copy).then_inc(cx_copied, 1)

            act.wait_ge(v_made, 1)
            nc.scalar.activation(vc.rearrange("p a b -> p (a b)"), ps_v, ACT.Copy).then_inc(v_copied, 1)
            todo = list(range(NK // 2))

            def some_cx(n):
                for _ in range(n):
                    copy_cx(todo.pop(0))

            some_cx(4)
            for n, (fn, row, rows) in enumerate(((ACT.Ln, 8, 2), (ACT.Tanh, 11, 1), (ACT.Ln, 8, 2))):
                act.wait_ge(act_asked, n + 1)
                nc.scalar.activation(sv[:, row:row + rows, :], sv[:, row:row + rows, :], fn).then_inc(act_done, 1)
                if n < 2:
                    some_cx(2 if n == 0 else 8)
            some_cx(len(todo))
            act.wait_ge(tangent_scales, 1)
            for k in range(NK):
                if k >= 2:
                    act.wait_ge(xt_ready, k - 1)
                nc.scalar.activation(fb[:, k % 2, :], hb, ACT.Copy, scale=sv[:, 14, k:k + 1]).then_inc(fb_ready, 1)

            def post_steps(p):
                row = p * L

                def copy():
                    act.wait_ge(block_multiplied, p * NK + NK)
                    if not (isinstance(p, int) and p == 0):
                        act.wait_ge(support_turned, p)
                    nc.scalar.activation(support_T[:], acc_of[0], ACT.Copy).then_inc(support_copied, 1)

                def squares():
                    act.wait_ge(relu_ready, p + 1)
                    nc.scalar.activation(sq1, support, ACT.Square).then_inc(u_squared, 1)
                    nc.scalar.activation(sq2, relu_u[:], ACT.Square).then_inc(relu_squared, 1)

                def tanh():
                    act.wait_ge(shrunk_ready, p + 1)
                    nc.scalar.activation(post[:, 28:32], post[:, 24:28], ACT.Tanh).then_inc(tanh_ready, 1)

                def normed():
                    act.wait_ge(norm2_ready, p + 1)
                    if isinstance(p, int) and p == NC - 1:
                        act.wait_ge(rest0_ready, 1)
                    for l in range(L):
                        dst = (h2[:, row + l, :] if isinstance(p, int) else
                               h2[:, bass.ds(row + l, 1), :].rearrange("p o d -> p (o d)"))
                        ins = nc.scalar.activation(dst, xk[:, l, :], ACT.Relu, bias=post[:, 36 + l:37 + l],
                                                   scale=post[:, 48 + l:49 + l])
                    ins.then_inc(h2_ready, 1)
                return {0: copy, 4: squares, 8: tanh, 13: normed}

            acc_of = [None]

            def signs(c, parity):
                number = isinstance(c, int)
                acc_of[0] = acc[1 - parity]
                steps = {} if number and c == 0 else post_steps(c - 1)
                mc = mask[:, c] if number else mask[:, bass.ds(c, 1)].rearrange("p o k i -> p (o k) i")
                if number and c == 1:
                    act.wait_ge(nl_stored, 16)
                for half in range(TH):
                    act.wait_ge(block_turned, c * NK + HB * (half + 1))
                    slots = half % HALVES * HB
                    nc.scalar.activation(mc[:, half * HB:(half + 1) * HB, :], turned[:, slots:slots + HB, :],
                                         ACT.Sign).then_inc(half_signed, 1)
                    if number and c == 0 and half == 8:
                        act.wait_ge(expo_asked, 1)
                        nc.scalar.activation(sv[:, 16:20, :], sv[:, 16:20, :], ACT.Exp).then_inc(expo_done, 1)
                    if half in steps:
                        steps[half]()
            chunked(act, signs)
            acc_of[0] = acc[1]
            last = post_steps(NC - 1)
            last[0]()
            last[4]()

            def edges(c, parity):
                number = isinstance(c, int)
                mc = mask[:, c] if number else mask[:, bass.ds(c, 1)].rearrange("p o k i -> p (o k) i")
                for g in range(NC):
                    if number and c == 0:
                        act.wait_ge(h2_ready, g + 1)
                        for k in range(g * L, g * L + L):
                            nc.scalar.activation(G[1][:, k, 0:D], h2[:, k, :], ACT.Copy,
                                                 scale=s1_col[:, k:k + 1]).then_inc(head_ready, 1)
                    if number and c == 0:
                        if g >= 3:
                            act.wait_ge(parts_used, g - 2)
                    elif number and c == 1 and g < 2:
                        act.wait_ge(edges_ready, NC)
                    elif g == 3:
                        act.wait_ge(rows_summed, c * L)
                    else:
                        act.wait_ge(parts_used, c * (NC - 1) + g - 3 if g > 3 else
                                    c * (NC - 1) - (NC - 1) + g + 5)
                    nc.scalar.activation(neg[slot(c, g)], mc[:, g * L:(g + 1) * L, :], ACT.Relu,
                                         scale=4.0).then_inc(edges_ready, 1)
                    if g == 0:
                        act.wait_ge(nl_loaded[parity], nl_count(c, parity))
                    for kk in range(HB, L):
                        k = g * L + kk
                        ins = nc.scalar.activation(pos[slot(c, g)][:, kk, :], nl[parity], ACT.Sign, scale=-1.0,
                                                   bias=r_col[:, k:k + 1])
                    ins.then_inc(signs_ready, 1)
                    if number and c == 0 and g in (1, 6):
                        last[8 if g == 1 else 13]()
                    if g == 2 and not (number and c == 0):
                        scale_rows(c - 1)
                    if g == NC // 2 and not (number and c == 0):
                        relu_rows(c - 1)

            def relu_rows(p):
                act.wait_ge(summed_read, p + 1)
                nc.scalar.activation(y, y, ACT.Relu).then_inc(y_relu, 1)

            def scale_rows(p):
                for t in range(L):
                    act.wait_ge(rows_summed, p * L + t + 1)
                    if not (isinstance(p, int) and p == 0 and t < 2):
                        act.wait_ge(rows_taken, p * L + t - 1)
                    nc.scalar.activation(neg_part[:, t % 2, :], ps[:, 2 * t, 0:GW], ACT.Copy,
                                         scale=cols(b_col, p * L + t, 1)).then_inc(neg_scaled, 1)
            chunked(act, edges)
            scale_rows(NC - 1)
            relu_rows(NC - 1)

        @block.vector
        def _(dve):
            v = nc.vector
            step = Steps(dve, dve_step)

            def affine0(l):
                dve.wait_ge(rstd0_ready, l + 1)
                v.scalar_tensor_tensor(out=cols_l(sv[:, 3, :], l), in0=by_l(mv0, l)[:, :, 0], scalar=-1.0,
                                       in1=cols_l(sv[:, 2, :], l), op0=ALU.mult, op1=ALU.mult).then_inc(
                    affine_ready, 1)

            for l in range(L):
                dve.wait_ge(x_in_sem[l], 16 * NQ)
                ks = range(l, NK, L)
                for k in ks:
                    ins = v.bn_stats(stats0[:, k, :], x_in[:, k, :])
                if l >= 1:
                    affine0(l - 1)
                step(ins)
                for k in ks:
                    ins = v.bn_aggr(mv0[:, k, :], stats0[:, k, :])
                step(ins)
                v.tensor_scalar(cols_l(sv[:, 0, :], l), by_l(mv0, l)[:, :, 1], LN_EPS, None, ALU.add).then_inc(
                    var0_ready, 1)
                if l == 0:
                    dve.wait_ge(weights_in, 16 * 3)
                    step(v.tensor_tensor(b_sq, bias_b, bias_b, ALU.mult))
                    step(v.reduce_sum(post[:, 0:1], b_sq, AX_X))
                    v.tensor_scalar(post[:, 0:1], post[:, 0:1], MIN_NORM2, None, ALU.max).then_inc(bias_summed, 1)
            affine0(L - 1)
            dve.wait_ge(bias_tanh, 1)
            step(v.scalar_tensor_tensor(out=post[:, 4:5], in0=post[:, 2:3], scalar=MAX_NORM, in1=post[:, 3:4],
                                        op0=ALU.min, op1=ALU.mult))
            v.tensor_scalar(hb_colv, b_colv, post[:, 4:5], None, ALU.mult).then_inc(bias_ready, 1)
            step(v.tensor_scalar(hb, bias_b, post[:, 4:5], None, ALU.mult))
            step(v.tensor_tensor(b_sq, hb, hb, ALU.mult))
            step(v.reduce_sum(post[:, 5:6], b_sq, AX_X))
            b2 = post[:, 5:6]
            dve.wait_ge(small_turned, 2)
            v.tensor_copy(WTb, ps_W[:, P:P + 1]).then_inc(wtb_made, 1)

            for u in range(NG + 2):
                if u < NG:
                    l, j, ks = groups[u]
                    dve.wait_ge(h_squared, u + 1)
                    v.reduce_sum(cols_l(sv[:, 5, :], l, j), by_l(x_in, l, j), AX_X)
                if u >= 2:
                    l, j, ks = groups[u - 2]
                    dve.wait_ge(mx_squared, u - 1)
                    ins = v.reduce_sum(cols_l(sv[:, 6, :], l, j), by_l(h, l, j), AX_X)
            step(ins)
            dve.wait_ge(mx_done, NG)
            step(v.tensor_copy(sv[:, 7, :], ps_mb))

            HN, MN, MB, P1, X2, T1, T2 = (sv[:, n, :] for n in (5, 6, 7, 10, 12, 13, 14))
            def artanh_over(n, inv, dst, cap, asked):
                lo, hi = sv[:, 8, :], sv[:, 9, :]
                p, q, s, m = sv[:, 15, :], sv[:, 20, :], sv[:, 21, :], sv[:, 22, :]
                step(v.tensor_scalar(p, n, cap, None, ALU.min))
                v.tensor_scalar(lo, p, 1.0, None, ALU.add)
                v.tensor_scalar(hi, p, -1.0, 1.0, ALU.mult, ALU.add).then_inc(act_asked, 1)
                step(v.tensor_tensor(q, p, p, ALU.mult))
                step(v.tensor_scalar(s, q, 1.0 / 13, None, ALU.mult))
                for c in (1 / 11, 1 / 9, 1 / 7, 1 / 5, 1 / 3):
                    step(v.scalar_tensor_tensor(out=s, in0=s, scalar=c, in1=q, op0=ALU.add, op1=ALU.mult))
                v.tensor_scalar(m, p, 0.3, None, ALU.is_lt)
                step(v.scalar_tensor_tensor(out=s, in0=s, scalar=1.0, in1=p, op0=ALU.add, op1=ALU.mult))
                dve.wait_ge(act_done, asked)
                step(v.tensor_tensor(lo, lo, hi, ALU.subtract))
                step(v.scalar_tensor_tensor(out=s, in0=lo, scalar=-0.5, in1=s, op0=ALU.mult, op1=ALU.add))
                step(v.tensor_tensor(s, s, m, ALU.mult))
                step(v.scalar_tensor_tensor(out=lo, in0=lo, scalar=0.5, in1=s, op0=ALU.mult, op1=ALU.add))
                step(v.tensor_tensor(dst, lo, inv, ALU.mult))

            v.tensor_scalar(sv[:, 5:7, :], sv[:, 5:7, :], MIN_NORM2, None, ALU.max).then_inc(roots_asked, 1)
            dve.wait_ge(roots_done, 2)
            artanh_over(HN, sv[:, 24, :], T1, ARTANH_CLIP, 1)
            v.tensor_tensor(sv[:, 11, :], T1, MN, ALU.mult).then_inc(act_asked, 1)
            dve.wait_ge(act_done, 2)
            step(v.tensor_scalar(P1, sv[:, 11, :], MAX_NORM, None, ALU.min))
            step(v.tensor_tensor(X2, P1, P1, ALU.mult))
            step(v.tensor_tensor(P1, P1, sv[:, 25, :], ALU.mult))
            XY = sv[:, 16, :]
            step(v.tensor_tensor(XY, P1, MB, ALU.mult))
            step(v.tensor_scalar(XY, XY, 2.0, 1.0, ALU.mult, ALU.add))
            A, B, DEN = sv[:, 17, :], sv[:, 18, :], sv[:, 19, :]
            v.tensor_scalar(A, XY, b2, None, ALU.add)
            v.tensor_scalar(B, X2, -1.0, 1.0, ALU.mult, ALU.add)
            step(v.scalar_tensor_tensor(out=DEN, in0=X2, scalar=b2, in1=XY, op0=ALU.mult, op1=ALU.add))
            step(v.tensor_scalar(DEN, DEN, 1e-15, None, ALU.max))
            step(v.reciprocal(DEN, DEN))
            v.tensor_tensor(B, B, DEN, ALU.mult)
            step(v.tensor_tensor(A, A, P1, ALU.mult))
            step(v.tensor_tensor(A, A, DEN, ALU.mult))
            step(v.tensor_tensor(T1, MN, A, ALU.mult))
            step(v.tensor_tensor(T1, T1, T1, ALU.mult))
            step(v.tensor_tensor(T2, A, B, ALU.mult))
            step(v.tensor_tensor(T2, T2, MB, ALU.mult))
            step(v.scalar_tensor_tensor(out=T1, in0=T2, scalar=2.0, in1=T1, op0=ALU.mult, op1=ALU.add))
            step(v.tensor_tensor(T2, B, B, ALU.mult))
            step(v.scalar_tensor_tensor(out=HN, in0=T2, scalar=b2, in1=T1, op0=ALU.mult, op1=ALU.add))
            v.tensor_scalar(HN, HN, MIN_NORM2, None, ALU.max).then_inc(roots_asked, 1)
            dve.wait_ge(roots_done, 4)
            artanh_over(HN, sv[:, 24, :], T1, MAX_NORM, 3)
            v.tensor_tensor(T2, B, T1, ALU.mult)
            v.tensor_tensor(T1, A, T1, ALU.mult).then_inc(tangent_scales, 1)
            dve.wait_ge(tangent_scales, 1)
            for k in range(NK):
                dve.wait_ge(fb_ready, k + 1)
                if k == 0:
                    dve.wait_ge(mx_copied, NC)
                v.scalar_tensor_tensor(out=xt[:, k, :], in0=mx[:, k, :], scalar=T1[:, k:k + 1], in1=fb[:, k % 2, :],
                                       op0=ALU.mult, op1=ALU.add).then_inc(xt_ready, 1)

            E1, E0, EA, EB = (sv[:, n, :] for n in (16, 17, 18, 19))
            R = post[:, 63:64]

            def left_right():
                lr = ps_lr.rearrange("p (k w) -> p w k", w=2)
                dve.wait_ge(lr_made, 1)
                dve.wait_ge(context_weights_in, 16 * 5)
                v.tensor_scalar(r_col[:], lr[:, 1], wlr[:, 3:4], None, ALU.add)
                step(v.tensor_scalar(l_col, lr[:, 0], wlr[:, 2:3], None, ALU.add))
                v.tensor_scalar(sv[:, 23, :], l_col, -1.0, None, ALU.mult).then_inc(nl_ready, 1)
                v.reduce_max(post[:, 62:63], r_col[:], AX_X).then_inc(rmax_part, 1)

            def exponents():
                dve.wait_ge(nl_turned, 1)
                v.tensor_copy(nlT[0:NK, :], ps_nl[0:NK, :]).then_inc(nl_copied, 1)
                dve.wait_ge(rmax_all, 1)
                v.tensor_scalar(EA, l_col, R, None, ALU.add)
                step(v.tensor_scalar(E1, r_col[:], R, None, ALU.subtract))
                v.tensor_scalar(E0, E1, SLOPE, None, ALU.mult)
                step(v.tensor_scalar(EB, EA, SLOPE, None, ALU.mult))
                step(v.tensor_tensor(sv[:, 13, :], EA, EB, ALU.max))
                v.tensor_tensor(EA, EA, sv[:, 13, :], ALU.subtract)
                v.tensor_tensor(EB, EB, sv[:, 13, :], ALU.subtract).then_inc(expo_asked, 1)

            def weights():
                dve.wait_ge(expo_done, 1)
                v.tensor_copy(a_col[:], EA)
                v.tensor_copy(b_col[:], EB)
                v.tensor_scalar(s1_col[:], E1, SCALE, None, ALU.mult)
                step(v.tensor_scalar(s0_col[:], E0, SCALE, None, ALU.mult))
            at_chunk_0 = {4: left_right, 12: exponents, 24: weights}

            POST = 6

            def post_steps(p):
                first = isinstance(p, int) and p == 0
                chain = Steps(dve, dve_step, p * POST + step.n)
                UI, RN, INV, F, VN, TH_, TF, CO = (post[:, a:b] for a, b in (
                    (8, 12), (12, 16), (16, 20), (20, 24), (24, 28), (28, 32), (32, 36), (56, 60)))

                def relu():
                    dve.wait_ge(support_turned, p + 1)
                    v.tensor_scalar(relu_u[:], support, 0.0, None, ALU.max).then_inc(relu_ready, 1)

                def sums():
                    dve.wait_ge(u_squared, p + 1)
                    v.reduce_sum(post[:, 0:4], sq1, AX_X)
                    dve.wait_ge(relu_squared, p + 1)
                    chain(v.reduce_sum(post[:, 4:8], sq2, AX_X))
                    v.tensor_scalar(post[:, 0:8], post[:, 0:8], MIN_NORM2, None, ALU.max).then_inc(sums_ready, 1)

                def shrink():
                    dve.wait_ge(norms_ready, p + 1)
                    chain(v.tensor_scalar(F, UI, ARTANH_RIM, 1.0, ALU.mult, ALU.min))
                    v.tensor_tensor(VN, F, RN, ALU.mult).then_inc(shrunk_ready, 1)

                def residual():
                    dve.wait_ge(tanh_ready, p + 1)
                    v.reciprocal(INV, VN)
                    chain(v.scalar_tensor_tensor(out=TF, in0=TH_, scalar=MAX_NORM, in1=F, op0=ALU.min, op1=ALU.mult))
                    chain(v.tensor_tensor(CO, TF, INV, ALU.mult))
                    dve.wait_ge(xk_loaded, p * (16 * NQ) + 16 * NQ)
                    for l in range(L):
                        ins = v.scalar_tensor_tensor(out=xk[:, l, :], in0=relu_u[:, l, :], scalar=CO[:, l:l + 1],
                                                     in1=xk[:, l, :], op0=ALU.mult, op1=ALU.add)
                    ins.then_inc(x1_ready, 1)

                def spread():
                    dve.wait_ge(x1_ready, p + 1)
                    for l in range(L):
                        ins = v.bn_stats(stats[:, l, :], xk[:, l, :])
                    chain(ins)
                    v.memset(post[:, 61:62], 0.0)
                    for l in range(L):
                        ins = v.bn_aggr(mv[:, l, :], stats[:, l, :])
                    chain(ins)
                    v.tensor_scalar(post[:, 40:44], mv[:, :, 1], LN_EPS, None, ALU.add).then_inc(var_ready, 1)

                def affine():
                    dve.wait_ge(std_ready, p + 1)
                    if not first:
                        dve.wait_ge(h2_ready, p)
                    v.scalar_tensor_tensor(out=post[:, 36:40], in0=mv[:, :, 0], scalar=-1.0, in1=post[:, 48:52],
                                           op0=ALU.mult, op1=ALU.mult).then_inc(norm2_ready, 1)
                    chain_len[0] = chain.n
                return {6: relu, 10: sums, 14: shrink, 18: residual, 21: spread, 25: affine}

            chain_len = [0]

            def turn(c, parity):
                number = isinstance(c, int)
                steps = at_chunk_0 if number and c == 0 else post_steps(c - 1)
                for k in range(NK):
                    g, l = k // L, k % L
                    if l == 0:
                        dve.wait_ge(adj_in[g % XSLOTS], c * (16 * NQ * NC // XSLOTS) + 16 * NQ * (g // XSLOTS + 1))
                    if not (number and c == 0 and k < TSLOTS):
                        dve.wait_ge(block_multiplied, c * NK + k - TSLOTS + 1)
                        if k % HB == 0:
                            dve.wait_ge(half_signed, c * TH + (k - TSLOTS) // HB + 1)
                    v.transpose(
                        turned[:, k % TSLOTS, :].rearrange("p (l b i) -> p b l i", l=L, b=NQ),
                        loaded[:, g % XSLOTS, :, l * Q:(l + 1) * Q].rearrange("p (b l) q -> p b l q", b=NQ)).then_inc(
                        block_turned, 1)
                    if k in steps:
                        steps[k]()
            chunked(dve, turn)
            last = [f for _, f in sorted(post_steps(NC - 1).items())]
            last.pop(0)()
            last.pop(0)()
            dve.wait_ge(block_multiplied, NC * NK)
            for w, s_col in ((0, s0_col), (1, s1_col)):
                ins = v.tensor_copy(G[w][:, :, 2 * D], s_col[:])
            ins.then_inc(weight_heads, 1)
            dve.wait_ge(weight_heads, 1)
            for w, s_col in ((0, s0_col), (1, s1_col)):
                ins = v.tensor_tensor(G[w][:, :, 2 * D + 1], s_col[:], G[w][:, :, 2 * D], ALU.subtract)
            ins.then_inc(weight_cols, 1)

            def compare(c, parity, g):
                dve.wait_ge(edges_ready, c * NC + g + 1)
                for kk in range(HB):
                    k = g * L + kk
                    ins = v.tensor_scalar(pos[slot(c, g)][:, kk, :], nl[parity], r_col[:, k:k + 1], -1.0,
                                          ALU.is_le, ALU.add)
                ins.then_inc(compared, 1)

            def split(c, parity):
                number = isinstance(c, int)
                dve.wait_ge(nl_loaded[parity], nl_count(c, parity))
                ahead = not (number and c == 0)
                if ahead:
                    compare(c, parity, 0)
                for g in range(NC):
                    pos_g, neg_g = pos[slot(c, g)], neg[slot(c, g)]
                    if not ahead:
                        compare(c, parity, g)
                        for k in range(g * L, g * L + L):
                            dve.wait_ge(head_ready, k + 1)
                            v.scalar_tensor_tensor(out=G[1][:, k, D:2 * D], in0=h2[:, k, :],
                                                   scalar=s1_col[:, k:k + 1], in1=G[1][:, k, 0:D],
                                                   op0=ALU.mult, op1=ALU.subtract).then_inc(rest_ready, 1)
                    dve.wait_ge(signs_ready, c * NC + g + 1)
                    dve.wait_ge(compared, c * NC + g + 1)
                    v.tensor_tensor(pos_g, pos_g, neg_g, ALU.add).then_inc(coded, 1)
                    if ahead and g + 1 < NC:
                        compare(c, parity, g + 1)
                    dve.wait_ge(coded, c * NC + g + 1)
                    v.tensor_scalar(neg_g, pos_g, 3.0, None, ALU.is_equal)
                    v.tensor_scalar(pos_g, pos_g, 4.0, None, ALU.is_ge).then_inc(parts_ready, 1)
                    if not ahead and g in (0, 1, 2, 5):
                        last.pop(0)()
                    if g == 1 and ahead:
                        take_rows(c - 1)

            def take_rows(p):
                if not (isinstance(p, int) and p == 0):
                    dve.wait_ge(summed_read, p)
                for t in range(L):
                    dve.wait_ge(neg_scaled, p * L + t + 1)
                    v.scalar_tensor_tensor(out=summed[:, t, :], in0=ps[:, 2 * t + 1, 0:GW],
                                           scalar=cols(a_col, p * L + t, 1), in1=neg_part[:, t % 2, :],
                                           op0=ALU.mult, op1=ALU.add).then_inc(rows_taken, 1)
                dve.wait_ge(rows_taken, p * L + L)
                v.tensor_tensor(post[:, 56:60], summed[:, :, 2 * D], summed[:, :, 2 * D + 1], ALU.add).then_inc(
                    weights_summed, 1)
                dve.wait_ge(weights_summed, p + 1)
                v.reciprocal(post[:, 52:56], post[:, 56:60]).then_inc(recip_ready, 1)

            chunked(dve, split)
            take_rows(NC - 1)


_INS = ['x', 'adj', 'L0_gnn_weight', 'L0_gnn_bias', 'L1_gnn_context', 'L1_gnn_W_common', 'L1_gnn_w_left',
        'L1_gnn_b_left', 'L1_gnn_w_right', 'L1_gnn_b_right']
_OUTS = [((4096, 128), 'float32')]


def kernel(**inputs):
    import numpy as _np
    import concourse.bacc as _bacc
    from concourse import mybir as _mybir
    from concourse.bass_utils import run_bass_kernel_spmd as _run

    nc = _bacc.Bacc("TRN2", target_bir_lowering=False, num_devices=1)
    arrays, args = {}, []
    for name in _INS:
        a = _np.ascontiguousarray(inputs[name])
        if a.ndim == 0 or name.endswith(("b_left", "b_right")):
            a = a.reshape(1, 1)
        arrays[f"in_{name}_dram"] = a
        args.append(nc.dram_tensor(f"in_{name}_dram", a.shape, _mybir.dt.from_np(a.dtype), kind="ExternalInput").ap())
    for i, (shape, dtype) in enumerate(_OUTS):
        dt = _mybir.dt.from_np(_np.dtype(dtype))
        args.append(nc.dram_tensor(f"out_{i}_dram", shape, dt, kind="ExternalOutput").ap())
    bass_two_graph_layers(nc, *args)
    r = _run(nc, [arrays], core_ids=[0])
    return r.results[0]["out_0_dram"]
```

```python
import math
from contextlib import ExitStack

import concourse.bass as bass
from concourse import mybir

F32 = mybir.dt.float32
F16 = mybir.dt.float16
BF16 = mybir.dt.bfloat16
I8 = mybir.dt.int8
ALU = mybir.AluOpType
ACT = mybir.ActivationFunctionType
AX_X = mybir.AxisListType.X
RMAX = bass.bass_isa.ReduceOp.max

P = 128
Q = 32
NQ = P // Q
L = 4
CH = L * P
XSLOTS = 4
HB = 2
HALVES = L // HB
TSLOTS = 4
XT_AHEAD = 4
BESIDE = 8

MIN_NORM2 = 1e-30
MAX_NORM = 1.0 - 1e-5
ARTANH_RIM = 6.103033822758835
ARTANH_CLIP = 1.0 - 1e-7
LN_EPS = 1e-5
SLOPE = 0.2
SCALE = 4096.0


class Steps:

    def __init__(self, eng, sem, base=0):
        self.eng, self.sem, self.base, self.n = eng, sem, base, 0

    def __call__(self, ins):
        self.n += 1
        ins.then_inc(self.sem, 1)
        self.eng.wait_ge(self.sem, self.base + self.n)


def bass_two_graph_layers(nc, x, adj, weight, bias, context, w_common, w_left, b_left, w_right, b_right, out):
    N, D = x.shape
    C = context.shape[1]
    NK = N // P
    NC = N // CH
    TH = NC * HALVES
    GW = 2 * D + 2
    assert D == P and NC % 2 == 0 and NC >= 4 and w_common.shape == (P, C)

    with ExitStack() as ctx:
        def sb(name, shape, dt):
            return ctx.enter_context(nc.sbuf_tensor(name, shape, dt))

        def sem(name):
            return ctx.enter_context(nc.semaphore(name))

        mask = sb("mask", [P, NC, NK, CH], I8)
        h2_room = sb("h2_room", [P, NK * D * 4], I8)
        XT_BYTES = NK * D * 4
        phase_1_bytes = XT_BYTES + XSLOTS * CH * L * 4 + TSLOTS * CH * 4
        phase_2_bytes = 2 * NK * GW * 2 + 3 * 2 * L * CH * 2
        room = sb("room", [P, max(phase_1_bytes, phase_2_bytes) + CH * 4], I8)
        relu_u = sb("relu_u", [P, L, D], F32)
        xk = sb("xk", [P, L, D], F32)
        ident = sb("ident", [P, P], F32)
        r_col = sb("r_col", [P, NK], F32)
        factors = sb("factors", [P, 4, NK], F32)
        a_col, b_col, s1_col, s0_col = (factors[:, n, :] for n in range(4))
        post = sb("post", [P, 64], F32)
        stats = sb("stats", [P, L, 6], F32)
        mv = sb("mv", [P, L, 2], F32)
        powers = sb("powers", [P, 2 * L], F32)
        euler = sb("euler", [P, 1], F32)
        constants = sb("constants", [P, 3], F32)

        def view(tensor, offset, shape, dt):
            size = {F32: 4, F16: 2, BF16: 2}[dt]
            n = 1
            for s in shape:
                n *= s
            v = tensor[:, offset:offset + n * size].bitcast(dt)
            if len(shape) == 2:
                v = v.rearrange("p (a b) -> p a b", a=shape[0])
            if len(shape) == 3:
                v = v.rearrange("p (a b c) -> p a b c", a=shape[0], b=shape[1])
            return v

        o = 0
        xt = view(room, o, [NK, D], F32)
        o += NK * D * 4
        loaded = view(room, o, [XSLOTS, L * NQ, L * Q], F32)
        o += XSLOTS * CH * L * 4
        turned = view(room, o, [TSLOTS, CH], F32)
        o = room.shape[1] - CH * 4
        support_T = view(room, o, [CH], F32)
        half_slot = L * CH * 2
        nl_at = XT_BYTES
        assert nl_at == 4 * half_slot and (NC - XSLOTS) % XSLOTS == 0
        nl_even = view(room, nl_at, [CH], F32)
        o = nl_at + CH * 4
        G = [None, None]
        for w in (0, 1):
            G[w] = view(room, o, [NK, GW], F16)
            o += NK * GW * 2
        places = [n * half_slot for n in range(4)] + [o, o + half_slot]
        pos, neg = ([view(room, at, [L, CH], BF16) for at in places[n::2]] for n in (0, 1))
        h2 = view(h2_room, 0, [NK, D], F32)
        o = 0
        summed = view(h2_room, o, [L, GW], F32)
        o += L * GW * 4
        neg_part = view(h2_room, o, [2, GW], F32)
        o += 2 * GW * 4
        y = view(h2_room, o, [L, D], F32)
        o += L * D * 4
        x1k = view(h2_room, o, [L, D], F32)
        nl = [nl_even, relu_u[:].rearrange("p l d -> p (l d)")]

        scratch = mask[:, :, :, :].rearrange("p c k i -> p (c k i)")
        place = [NC * NK * CH]
        for n, slots in enumerate((pos, neg, pos, neg)):
            slots.append(view(scratch, n * L * CH * 2, [L, CH], BF16))

        def tmp(shape):
            n = 4
            for d in shape:
                n *= d
            place[0] -= n
            assert place[0] >= NK * CH
            return view(scratch, place[0], shape, F32)

        cx, v_rows, w_wide, lr, extreme = tmp([NK, C]), tmp([2, C]), tmp([2, P]), tmp([2, NK]), tmp([NK])
        neg_l, wlr, Wc = tmp([NK]), tmp([4]), tmp([C])
        x_in, h, mx = tmp([NK, D]), tmp([NK, D]), tmp([NK, D + 1])
        W_in, WT, b_colv, hb_colv = tmp([D]), tmp([D + 1]), tmp([1]), tmp([1])
        bias_b, hb, b_sq = tmp([D]), tmp([D]), tmp([D])
        hT, fb = tmp([2, L * P]), tmp([XT_AHEAD, D])
        stats0, mv0 = tmp([NK, 6]), tmp([NK, 2])
        sv, table_cells = tmp([26, NK]), tmp([5])
        products = x_in.rearrange("p k d -> p (k d)")[:, 0:BESIDE * C].rearrange("p (k c) -> p k c", c=C)

        ps = ctx.enter_context(nc.psum_tensor("ps", [P, 8, 512], F32))
        acc = [ps[:, 0, :], ps[:, 1, :]]
        support, sq1, sq2 = (ps[:, n, :].rearrange("p (l d) -> p l d", l=L) for n in (5, 6, 7))
        ps_hT = [ps[:, 0, :], ps[:, 1, :]]
        ps_mx = [ps[:, n:n + 2, 0:2 * (D + 1)].rearrange("p n (a d) -> p n a d", a=2) for n in (2, 6)]
        ps_v, ps_W = ps[:, 4, :], ps[:, 5, 0:P + 1]

        nl_dram = nc.dram_tensor("neg_left", (NK, P), F32, kind="Internal").ap()

        weights_in, context_weights_in = sem("weights_in"), sem("context_weights_in")
        x_in_sem, cx_in = [sem(f"x_loaded_{l}") for l in range(L)], [sem(f"context_loaded_{l}") for l in range(L)]
        zeroed, ident_made, powers_made = sem("ident_zeroed"), sem("ident_made"), sem("powers_made")
        adj_in = [sem(f"adj_loaded_{s}") for s in range(XSLOTS)]
        block_turned, block_multiplied, half_signed = sem("block_turned"), sem("block_multiplied"), sem("half_signed")
        dve_step, pool_step, weight_heads, weights_summed = (sem("dve_step"), sem("pool_step"), sem("weight_heads"),
                                                            sem("weights_summed"))
        bias_summed, bias_powers, bias_tanh, bias_ready = (sem("bias_summed"), sem("bias_powers"), sem("bias_tanh"),
                                                           sem("bias_ready"))
        small_turned, wt_copied, w_widened = sem("small_turned"), sem("wt_copied"), sem("w_widened")
        var0_ready, rstd0_ready, affine_ready, h_ready = (sem("var0_ready"), sem("rstd0_ready"), sem("affine_ready"),
                                                          sem("h_ready"))
        hT_turned, hT_copied, h_squared = sem("hT_turned"), sem("hT_copied"), sem("h_squared")
        mx_done, mx_squared, mx_copied = sem("mx_done"), sem("mx_squared"), sem("mx_copied")
        roots_asked, roots_done = sem("roots_asked"), sem("roots_done")
        act_asked, act_done = sem("act_asked"), sem("act_done")
        tangent_scales, fb_ready, xt_ready = sem("tangent_scales"), sem("fb_ready"), sem("xt_ready")
        v_made, v_copied = sem("v_made"), sem("v_copied")
        beside_step, rmax_all, nl_stored, factors_ready = (sem("beside_step"), sem("rmax_all"), sem("nl_stored"),
                                                           sem("factors_ready"))
        support_copied, support_turned = sem("support_copied"), sem("support_turned")
        relu_ready, u_squared, relu_squared = sem("relu_ready"), sem("u_squared"), sem("relu_squared")
        sums_ready, norms_ready = sem("sums_ready"), sem("norms_ready")
        shrunk_ready, tanh_ready = sem("shrunk_ready"), sem("tanh_ready")
        xk_loaded, x1_ready, x1_stored = sem("xk_loaded"), sem("x1_ready"), sem("x1_stored")
        var_ready, std_ready, norm2_ready, h2_ready = (sem("var_ready"), sem("std_ready"), sem("norm2_ready"),
                                                       sem("h2_ready"))
        nl_loaded = [sem("nl_loaded_even"), sem("nl_loaded_odd")]
        weight_cols = sem("weight_cols")
        head_ready, rest_ready, rest0_ready = sem("head_ready"), sem("rest_ready"), sem("rest0_ready")
        edges_ready, signs_ready, compared, coded = (sem("edges_ready"), sem("signs_ready"), sem("compared"),
                                                     sem("coded"))
        parts_ready, parts_used = sem("parts_ready"), sem("parts_used")
        rows_summed, neg_scaled, rows_taken = sem("rows_summed"), sem("neg_scaled"), sem("rows_taken")
        recip_ready, summed_read, final_step = sem("recip_ready"), sem("summed_read"), sem("final_step")
        y_relu, rest0_scaled, head0_ready = sem("y_relu"), sem("rest0_scaled"), sem("head0_ready")
        x1_loaded, y_ready, out_stored = sem("x1_loaded"), sem("y_ready"), sem("out_stored")

        def nodes(t):
            return t.rearrange("(s b l q) d -> s b q l d", b=NQ, l=L, q=Q)

        x_n, out_n = nodes(x), nodes(out)
        x_l, cx_l = (t.rearrange("(s b l q) d -> l b q s d", b=NQ, l=L, q=Q) for t in (x, context))
        adj_n = adj.rearrange("(s r p) (g b j) -> s g b p r j", r=CH // Q, p=Q, b=NQ, j=L * Q)

        def pick(view_, c):
            if isinstance(c, int):
                return view_[c]
            v = view_[bass.ds(c, 1)]
            names = "abdefg"[:len(v.shape) - 1]
            return v.rearrange(f"z {' '.join(names)} -> (z {names[0]}) {' '.join(names[1:])}")

        def chunked(eng, chunk):
            chunk(0, 0)
            chunk(1, 1)
            with eng.Fori(1, NC // 2) as pair:
                chunk(pair * 2, 0)
                chunk(pair * 2 + 1, 1)

        def cols(t, start, n):
            return t[:, start:start + n] if isinstance(start, int) else t[:, bass.ds(start, n)]

        def nl_count(c, parity):
            if isinstance(c, int):
                return 16 * (c // 2 + 1)
            return c * 8 + (8 if parity else 16)

        def slot(c, g):
            return g % 3 if isinstance(c, int) and c == 0 else (3, 4, 0, 1)[g % 4]

        def compared_by_dve(c, g):
            return L if isinstance(c, int) and c == 0 and g == 0 else HB

        def by_l(t, l, j=None):
            v = t.rearrange("p (s l) d -> p l s d", l=L)[:, l]
            return v if j is None else v[:, j * L:(j + 1) * L]

        def cols_l(t, l, j=None):
            v = t.rearrange("p (s l) -> p l s", l=L)[:, l]
            return v if j is None else v[:, j * L:(j + 1) * L]

        groups = [(u // 2, u % 2, [L * s + u // 2 for s in range(L * (u % 2), L * (u % 2) + L)])
                  for u in range(NK // L)]
        NG = len(groups)
        assert NK // L // 2 == L

        block = ctx.enter_context(nc.Block())

        @block.sync
        def _(sp):
            def load_nodes(t, src, into):
                for l in range(L):
                    for b in range(NQ):
                        sp.dma_start(by_l(t, l)[b * Q:(b + 1) * Q], src[l, b]).then_inc(into[l], 16)
            load_nodes(x_in, x_l, x_in_sem)

            def store_x1(p):
                sp.wait_ge(x1_ready, p + 1)
                os = pick(out_n, p)
                for b in range(NQ):
                    sp.dma_start(os[b], xk[b * Q:(b + 1) * Q]).then_inc(x1_stored, 16)

            def load_x(p):
                if not (isinstance(p, int) and p == 0):
                    sp.wait_ge(x1_stored, p * (16 * NQ))
                    sp.wait_ge(h2_ready, p)
                xs = pick(x_n, p)
                for b in range(NQ):
                    sp.dma_start(xk[b * Q:(b + 1) * Q], xs[b]).then_inc(xk_loaded, 16)

            def load(c, _):
                rows = pick(adj_n, c)
                for g in range(NC):
                    if not (isinstance(c, int) and c == 0 and g < XSLOTS):
                        sp.wait_ge(block_turned, c * NK + L * (g - XSLOTS + 1))
                    for b in range(NQ):
                        sp.dma_start(loaded[b * Q:(b + 1) * Q, g % XSLOTS], rows[g, b]).then_inc(
                            adj_in[g % XSLOTS], 16)
                    if isinstance(c, int) and c == 0 and g == XSLOTS - 1:
                        load_nodes(cx, cx_l, cx_in)
                    if g == 1 and not (isinstance(c, int) and c < 2):
                        store_x1(c - 2)
                    if g == 3 and not (isinstance(c, int) and c < 1):
                        load_x(c - 1)

            def neg_left_row(c, parity):
                sp.dma_start(nl[parity], (nl_dram[c * L:(c + 1) * L] if isinstance(c, int) else
                                          nl_dram[bass.ds(c * L, L)]).rearrange("(a l) p -> a (l p)", a=1)
                             .broadcast_to([P, CH])).then_inc(nl_loaded[parity], 16)

            chunked(sp, load)
            sp.wait_ge(nl_stored, 16)
            sp.wait_ge(block_turned, NC * NK - (XSLOTS - 1) * L)
            neg_left_row(0, 0)
            store_x1(NC - 2)
            load_x(NC - 1)

            def rows_out(p):
                os = pick(out_n, p)
                for b in range(NQ):
                    sp.dma_start(x1k[b * Q:(b + 1) * Q], os[b]).then_inc(x1_loaded, 16)
                sp.wait_ge(y_ready, p + 1)
                for b in range(NQ):
                    sp.dma_start(os[b], y[b * Q:(b + 1) * Q]).then_inc(out_stored, 16)

            def chunk_of_phase_2(c, parity):
                sp.wait_ge(parts_ready, c * NC - NC)
                neg_left_row(c, parity)
                rows_out(c - 2)

            store_x1(NC - 1)
            neg_left_row(1, 1)
            sp.wait_ge(x1_stored, NC * 16 * NQ)
            sp.wait_ge(rest_ready, NK)
            sp.wait_ge(rest0_ready, NC)
            with sp.Fori(1, NC // 2) as pair:
                chunk_of_phase_2(pair * 2, 0)
                chunk_of_phase_2(pair * 2 + 1, 1)
            rows_out(NC - 2)
            for b in range(NQ):
                sp.dma_start(x1k[b * Q:(b + 1) * Q], out_n[NC - 1, b]).then_inc(x1_loaded, 16)
            for l in range(0, L, 2):
                sp.wait_ge(y_ready, NC + l // 2)
                for b in range(NQ):
                    sp.dma_start(out_n[NC - 1, b][:, l:l + 2], y[b * Q:(b + 1) * Q, l:l + 2]).then_inc(out_stored, 16)
            sp.wait_ge(out_stored, (NC + 1) * 16 * NQ)

        @block.gpsimd
        def _(pool):
            nc.gpsimd.memset(euler[:], math.e)
            for n, value in enumerate((SLOPE, SCALE, 0.0)):
                nc.gpsimd.memset(constants[:, n:n + 1], value)
            nc.gpsimd.memset(powers[:, 0:L], -0.5)
            nc.gpsimd.memset(powers[:, L:2 * L], 0.5).then_inc(powers_made, 1)
            nc.gpsimd.memset(ident[:], 0.0).then_inc(zeroed, 1)
            pool.wait_ge(zeroed, 1)
            nc.gpsimd.affine_select(out=ident[:], in_=ident[:], compare_op=ALU.not_equal, fill=1.0, base=0,
                                    pattern=[[-1, P]], channel_multiplier=1).then_inc(ident_made, 1)
            pool.dma_start(Wc, w_common).then_inc(context_weights_in, 16)
            for n, w in enumerate((w_left, w_right)):
                pool.dma_start(wlr[:, n:n + 1], w.rearrange("(d a) -> d a", a=1)).then_inc(context_weights_in, 16)
            for n, w in enumerate((b_left, b_right)):
                pool.dma_start(wlr[:, 2 + n:3 + n], w.broadcast_to([P, 1])).then_inc(context_weights_in, 16)
            pool.wait_ge(powers_made, 1)
            inv_root, root = (powers[:, n:n + 1] for n in (0, L))

            def power(dst, src, exponent):
                n = src.shape[1]
                return nc.gpsimd.tensor_tensor(dst, src, exponent.broadcast_to([P, n]), ALU.pow)

            def square_h(u):
                l, j, ks = groups[u]
                pool.wait_ge(h_ready, L * (u + 1))
                nc.gpsimd.tensor_tensor(by_l(x_in, l, j), by_l(h, l, j), by_l(h, l, j), ALU.mult).then_inc(h_squared, 1)

            for l in range(L):
                pool.wait_ge(var0_ready, l + 1)
                power(cols_l(sv[:, 2, :], l), cols_l(sv[:, 0, :], l), inv_root).then_inc(rstd0_ready, 1)
                if l == 0:
                    pool.wait_ge(bias_summed, 1)
                    power(post[:, 1:2], post[:, 0:1], root)
                    power(post[:, 3:4], post[:, 0:1], inv_root).then_inc(bias_powers, 1)
                if 0 < l < L - 1:
                    square_h(l - 1)
            for u in range(NG + 1):
                if L - 2 <= u < NG:
                    square_h(u)
                if u >= 2 and u % 2 == 0:
                    l, j, ks = groups[u - 2]
                    pool.wait_ge(mx_copied, u - 1)
                    pool.wait_ge(h_squared, u - 1)
                    got = by_l(mx, l, j)[:, :, 0:D]
                    nc.gpsimd.tensor_tensor(by_l(h, l, j), got, got, ALU.mult).then_inc(mx_squared, 1)

            pool.wait_ge(context_weights_in, 16 * 5)
            nc.gpsimd.tensor_copy(w_wide, wlr[:, 0:2].unsqueeze(2).broadcast_to([P, 2, P])).then_inc(w_widened, 1)

            side, tt = Steps(pool, beside_step), nc.gpsimd.tensor_tensor

            def left_or_right(w, part):
                ks = slice(part * BESIDE, (part + 1) * BESIDE)
                if w == 0 and part == 0:
                    pool.wait_ge(v_copied, 1)
                    pool.wait_ge(roots_asked, 1)
                    for l in range(L):
                        pool.wait_ge(cx_in[l], 16 * NQ)
                side(nc.gpsimd.tensor_tensor(products, cx[:, ks, :],
                                             v_rows[:, w, :].unsqueeze(1).broadcast_to([P, BESIDE, C]), ALU.mult))
                n = C // 2
                while n:
                    dst = products[:, :, 0:n] if n > 1 else lr[:, w, ks].unsqueeze(2)
                    side(nc.gpsimd.tensor_tensor(dst, products[:, :, 0:n], products[:, :, n:2 * n], ALU.add))
                    n //= 2

            def sums_and_rows():
                side(tt(r_col[:], lr[:, 1, :], wlr[:, 3:4].broadcast_to([P, NK]), ALU.add))
                side(tt(lr[:, 0, :], lr[:, 0, :], wlr[:, 2:3].broadcast_to([P, NK]), ALU.add))
                side(tt(neg_l, constants[:, 2:3].broadcast_to([P, NK]), lr[:, 0, :], ALU.subtract))
                pool.dma_start(nl_dram.rearrange("k p -> p k"), neg_l, allow_slow_non_contiguous=True).then_inc(
                    nl_stored, 16)

            def largest():
                for k in range(1, NK):
                    so_far = r_col[:, 0:1] if k == 1 else extreme[:, k % 2:k % 2 + 1]
                    side(nc.gpsimd.tensor_scalar(extreme[:, 1 - k % 2:2 - k % 2], r_col[:, k:k + 1], so_far, None,
                                                 ALU.max))
                nc.gpsimd.partition_all_reduce(extreme[:, 2:3], extreme[:, NK % 2:NK % 2 + 1], P, RMAX).then_inc(
                    rmax_all, 1)
                pool.wait_ge(rmax_all, 1)

            def exponents():
                R = extreme[:, 2:3].broadcast_to([P, NK])
                pool.wait_ge(nl_stored, 16)
                side(tt(a_col, lr[:, 0, :], R, ALU.add))
                side(tt(s1_col, r_col[:], R, ALU.subtract))
                side(tt(b_col, a_col, constants[:, 0:1].broadcast_to([P, NK]), ALU.mult))
                side(tt(s0_col, s1_col, constants[:, 0:1].broadcast_to([P, NK]), ALU.mult))
                nc.gpsimd.tensor_scalar(lr[:, 0, :], a_col, 0.0, None, ALU.max)
                side(nc.gpsimd.tensor_scalar(extreme, a_col, 0.0, SLOPE, ALU.min, ALU.mult))
                side(tt(lr[:, 0, :], lr[:, 0, :], extreme, ALU.add))
                side(tt(a_col, a_col, lr[:, 0, :], ALU.subtract))
                side(tt(b_col, b_col, lr[:, 0, :], ALU.subtract))

            def exponentials(n):
                two = factors[:, 2 * n:2 * n + 2, :].rearrange("p a k -> p (a k)")
                side(nc.gpsimd.tensor_tensor(two, euler[:].broadcast_to([P, 2 * NK]), two, ALU.pow))
                if n == 1:
                    nc.gpsimd.tensor_tensor(two, two, constants[:, 1:2].broadcast_to([P, 2 * NK]), ALU.mult).then_inc(
                        factors_ready, 1)
            parts = [(left_or_right, (w, part)) for w in range(2) for part in range(NK // BESIDE)]
            parts += [(sums_and_rows, ()), (largest, ()), (exponents, ()), (exponentials, (0,)),
                      (exponentials, (1,))]

            def beside(n=1):
                for _ in range(n):
                    if parts:
                        f, args = parts.pop(0)
                        f(*args)
            beside(4)

            def norms(p):
                pool.wait_ge(sums_ready, p + 1)
                nc.gpsimd.tensor_tensor(post[:, 8:16], post[:, 0:8], powers[:], ALU.pow).then_inc(norms_ready, 1)

            def inverse_std(p):
                pool.wait_ge(var_ready, p + 1)
                nc.gpsimd.tensor_tensor(post[:, 48:52], post[:, 40:44], powers[:, 0:L], ALU.pow).then_inc(std_ready, 1)

            for p in range(5):
                norms(p)
                if p < 4:
                    beside()
                inverse_std(p)
                beside()
            with pool.Fori(5, NC - 1) as p:
                norms(p)
                inverse_std(p)

            pool.wait_ge(weight_cols, 1)
            for g in range(NC):
                ks, place_of = (slice(n * L, n * L + L) for n in (g, (g - 1) % NC))
                scaled, head, rest = h2[:, place_of, :], G[0][:, ks, 0:D], G[0][:, ks, D:2 * D]
                pool.wait_ge(h2_ready, g + 1)
                if g:
                    pool.wait_ge(rest_ready, g * L)
                weight_0 = s0_col[:, ks].unsqueeze(2).broadcast_to([P, L, D])
                nc.gpsimd.tensor_tensor(scaled, h2[:, ks, :], weight_0, ALU.mult).then_inc(rest0_scaled, 1)
                nc.gpsimd.tensor_tensor(head, h2[:, ks, :], weight_0, ALU.mult).then_inc(head0_ready, 1)
                pool.wait_ge(rest0_scaled, g + 1)
                pool.wait_ge(head0_ready, g + 1)
                nc.gpsimd.tensor_tensor(rest, scaled, head, ALU.subtract).then_inc(rest0_ready, 1)
                if g == 1:
                    norms(NC - 1)
                if g == 4:
                    inverse_std(NC - 1)

            def last_steps(c, parity):
                step = Steps(pool, pool_step, c)
                pool.wait_ge(recip_ready, c + 1)
                if not (isinstance(c, int) and c == 0):
                    pool.wait_ge(out_stored, c * (16 * NQ))
                step(nc.gpsimd.tensor_tensor(y, summed[:, :, 0:D], summed[:, :, D:2 * D], ALU.add))
                ins = nc.gpsimd.tensor_tensor(y, y, post[:, 52:52 + L].unsqueeze(2).broadcast_to([P, L, D]), ALU.mult)
                ins.then_inc(summed_read, 1)
                pool.wait_ge(y_relu, c + 1)
                pool.wait_ge(x1_loaded, c * (16 * NQ) + 16 * NQ)
                nc.gpsimd.tensor_tensor(y, y, x1k, ALU.add).then_inc(y_ready, 1)
            last_steps(0, 0)
            last_steps(1, 1)
            with pool.Fori(1, NC // 2 - 1) as pair:
                last_steps(pair * 2, 0)
                last_steps(pair * 2 + 1, 1)
            last_steps(NC - 2, 0)

        @block.tensor
        def _(pe):
            pe.wait_ge(ident_made, 1)
            pe.wait_ge(weights_in, 16 * 3)
            pe.transpose(ps_W[:, 0:P], W_in, ident[:]).then_inc(small_turned, 1)
            pe.wait_ge(bias_ready, 1)
            pe.matmul(ps_W[:, P:P + 1], W_in, hb_colv, start=True, stop=True).then_inc(small_turned, 1)
            for u in range(NG + 1):
                if u < NG:
                    pe.wait_ge(h_ready, L * (u + 1))
                    if u >= 2:
                        pe.wait_ge(hT_copied, u - 1)
                    for n, k in enumerate(groups[u][2]):
                        mm = pe.transpose(ps_hT[u % 2][:, n * P:(n + 1) * P], h[:, k, :], ident[:])
                    mm.then_inc(hT_turned, 1)
                if u >= 1:
                    t = u - 1
                    pe.wait_ge(hT_copied, t + 1)
                    if t == 0:
                        pe.wait_ge(wt_copied, 1)
                    if t >= 2:
                        pe.wait_ge(mx_copied, t - 1)
                    for n, k in enumerate(groups[t][2]):
                        lhs = hT[:, t % 2, n * P:(n + 1) * P]
                        mm = pe.matmul(ps_mx[t % 2][:, n // 2, n % 2, :], lhs, WT, start=True, stop=True)
                    mm.then_inc(mx_done, 1)
            pe.wait_ge(w_widened, 1)
            for w in range(2):
                mm = pe.matmul(ps_v[:, w * C:(w + 1) * C], w_wide[:, w, :], Wc, start=True, stop=True)
            mm.then_inc(v_made, 1)
            def turn_support(p):
                pe.wait_ge(support_copied, p + 1)
                if not (isinstance(p, int) and p == 0):
                    pe.wait_ge(relu_ready, p)
                    pe.wait_ge(u_squared, p)
                for l in range(L):
                    mm = pe.transpose(support[:, l, :], support_T[:, l * P:(l + 1) * P], ident[:])
                mm.then_inc(support_turned, 1)

            def product(c, parity):
                number = isinstance(c, int)
                if not number or c >= 2:
                    pe.wait_ge(support_copied, c - 1)
                for k in range(NK):
                    pe.wait_ge(block_turned, c * NK + k + 1)
                    if number and c == 0:
                        pe.wait_ge(xt_ready, k + 1)
                    pe.matmul(acc[parity], xt[:, k, :], turned[:, k % TSLOTS, :],
                              start=(k == 0), stop=(k == NK - 1)).then_inc(block_multiplied, 1)
                    if k == 2 and not (number and c == 0):
                        turn_support(c - 1)
            chunked(pe, product)
            turn_support(NC - 1)

            def attend(c, parity):
                number = isinstance(c, int)
                for g in range(NC):
                    pe.wait_ge(parts_ready, c * NC + g + 1)
                    for t in range(L):
                        if g == 0 and not (number and c == 0):
                            pe.wait_ge(rows_taken, c * L + t - L + 1)
                        if g == 0 and number and c == 0:
                            if t == 0:
                                pe.wait_ge(weight_cols, 1)
                            if t == 2:
                                pe.wait_ge(sums_ready, NC)
                        for kk in range(L):
                            k = g * L + kk
                            if number and c == 0 and t == 0:
                                pe.wait_ge(rest_ready, k + 1)
                                pe.wait_ge(rest0_ready, g + 1)
                            for w, part in ((0, neg), (1, pos)):
                                mm = pe.matmul(ps[:, 2 * t + w, 0:GW], part[slot(c, g)][:, kk, t * P:(t + 1) * P],
                                               G[w][:, k, :], start=(k == 0), stop=(k == NK - 1))
                        if g == NC - 1:
                            mm.then_inc(rows_summed, 1)
                        elif t == L - 1:
                            mm.then_inc(parts_used, 1)
            chunked(pe, attend)

        @block.scalar
        def _(act):
            act.dma_start(W_in, weight).then_inc(weights_in, 16)
            act.dma_start(b_colv, bias.rearrange("(d a) -> d a", a=1)).then_inc(weights_in, 16)
            act.dma_start(bias_b, bias.rearrange("(a d) -> a d", a=1).broadcast_to([P, D])).then_inc(weights_in, 16)

            def copy_hT(u):
                act.wait_ge(hT_turned, u + 1)
                if u >= 2:
                    act.wait_ge(mx_done, u - 1)
                nc.scalar.activation(hT[:, u % 2, :], ps_hT[u % 2], ACT.Copy).then_inc(hT_copied, 1)

            def copy_mx(u):
                l, j, ks = groups[u]
                act.wait_ge(mx_done, u + 1)
                nc.scalar.activation(by_l(mx, l, j).rearrange("p (n a) d -> p n a d", a=2), ps_mx[u % 2],
                                     ACT.Copy).then_inc(mx_copied, 1)

            for u, (l, j, ks) in enumerate(groups):
                act.wait_ge(affine_ready, l + 1)
                for k in ks:
                    nc.scalar.activation(h[:, k, :], x_in[:, k, :], ACT.Relu, bias=sv[:, 3, k:k + 1],
                                         scale=sv[:, 2, k:k + 1]).then_inc(h_ready, 1)
                if u == 0:
                    act.wait_ge(bias_powers, 1)
                    nc.scalar.activation(post[:, 2:3], post[:, 1:2], ACT.Tanh).then_inc(bias_tanh, 1)
                if u == 1:
                    act.wait_ge(small_turned, 2)
                    nc.scalar.activation(WT, ps_W, ACT.Copy).then_inc(wt_copied, 1)
                if u >= 1:
                    copy_hT(u - 1)
                if u >= 2:
                    copy_mx(u - 2)
            copy_hT(NG - 1)
            copy_mx(NG - 2)
            copy_mx(NG - 1)

            act.wait_ge(powers_made, 1)
            for n, (asked, count, fn, row, rows, done) in enumerate((
                    (roots_asked, 1, ACT.Sqrt, 5, 2, roots_done), (act_asked, 1, ACT.Ln, 8, 2, act_done),
                    (act_asked, 2, ACT.Tanh, 11, 1, act_done), (roots_asked, 2, ACT.Sqrt, 5, 1, roots_done),
                    (act_asked, 3, ACT.Ln, 8, 2, act_done))):
                nc.scalar.activation(table_cells[:, n:n + 1], powers[:, L:L + 1], fn)
                act.wait_ge(asked, count)
                nc.scalar.activation(sv[:, row:row + rows, :], sv[:, row:row + rows, :], fn).then_inc(done, 1)
                if n == 0:
                    act.wait_ge(v_made, 1)
                    nc.scalar.activation(v_rows.rearrange("p a b -> p (a b)"), ps_v, ACT.Copy).then_inc(v_copied, 1)

            def bias_part(k):
                if k >= XT_AHEAD:
                    act.wait_ge(xt_ready, k - XT_AHEAD + 1)
                nc.scalar.activation(fb[:, k % XT_AHEAD, :], hb, ACT.Copy, scale=sv[:, 14, k:k + 1]).then_inc(
                    fb_ready, 1)
            act.wait_ge(tangent_scales, 1)
            for k in range(XT_AHEAD):
                bias_part(k)

            def post_steps(p):
                row = p * L

                def copy():
                    act.wait_ge(block_multiplied, p * NK + NK)
                    if not (isinstance(p, int) and p == 0):
                        act.wait_ge(support_turned, p)
                    nc.scalar.activation(support_T[:], acc_of[0], ACT.Copy).then_inc(support_copied, 1)

                def squares():
                    act.wait_ge(relu_ready, p + 1)
                    nc.scalar.activation(sq1, support, ACT.Square).then_inc(u_squared, 1)
                    nc.scalar.activation(sq2, relu_u[:], ACT.Square).then_inc(relu_squared, 1)

                def tanh():
                    act.wait_ge(shrunk_ready, p + 1)
                    nc.scalar.activation(post[:, 28:32], post[:, 24:28], ACT.Tanh).then_inc(tanh_ready, 1)

                def normed():
                    act.wait_ge(norm2_ready, p + 1)
                    if isinstance(p, int) and p == NC - 1:
                        act.wait_ge(rest0_ready, 1)
                    for l in range(L):
                        dst = (h2[:, row + l, :] if isinstance(p, int) else
                               h2[:, bass.ds(row + l, 1), :].rearrange("p o d -> p (o d)"))
                        ins = nc.scalar.activation(dst, xk[:, l, :], ACT.Relu, bias=post[:, 36 + l:37 + l],
                                                   scale=post[:, 48 + l:49 + l])
                    ins.then_inc(h2_ready, 1)
                return {0: copy, 4: squares, 8: tanh, 15: normed}

            acc_of = [None]

            def signs(c, parity):
                number = isinstance(c, int)
                acc_of[0] = acc[1 - parity]
                steps = {} if number and c == 0 else post_steps(c - 1)
                mc = mask[:, c] if number else mask[:, bass.ds(c, 1)].rearrange("p o k i -> p (o k) i")
                for half in range(TH):
                    act.wait_ge(block_turned, c * NK + HB * (half + 1))
                    slots = half % HALVES * HB
                    nc.scalar.activation(mc[:, half * HB:(half + 1) * HB, :], turned[:, slots:slots + HB, :],
                                         ACT.Sign).then_inc(half_signed, 1)
                    if number and c == 0:
                        for k in range(XT_AHEAD + half * HB, min(NK, XT_AHEAD + (half + 1) * HB)):
                            bias_part(k)
                    if half in steps:
                        steps[half]()
            chunked(act, signs)
            acc_of[0] = acc[1]
            last = post_steps(NC - 1)
            last[0]()
            act.wait_ge(half_signed, NC * TH)

            def heads(g):
                act.wait_ge(h2_ready, g + 1)
                for k in range(g * L, g * L + L):
                    nc.scalar.activation(G[1][:, k, 0:D], h2[:, k, :], ACT.Copy,
                                         scale=s1_col[:, k:k + 1]).then_inc(head_ready, 1)

            def edges(c, parity):
                number = isinstance(c, int)
                mc = mask[:, c] if number else mask[:, bass.ds(c, 1)].rearrange("p o k i -> p (o k) i")
                for g in range(NC):
                    if number and c == 0 and g:
                        heads(g)
                    if number and c == 0:
                        if g >= 3:
                            act.wait_ge(parts_used, g - 2)
                    elif number and c == 1 and g < 2:
                        act.wait_ge(edges_ready, NC)
                    elif g == 3:
                        act.wait_ge(rows_summed, c * L)
                    else:
                        act.wait_ge(parts_used, c * (NC - 1) + g - 3 if g > 3 else
                                    c * (NC - 1) - (NC - 1) + g + 5)
                    nc.scalar.activation(neg[slot(c, g)], mc[:, g * L:(g + 1) * L, :], ACT.Relu,
                                         scale=4.0).then_inc(edges_ready, 1)
                    if g == (1 if number else 2) and not (number and c == 0):
                        scale_rows(c - 1)
                    if g == 0:
                        act.wait_ge(nl_loaded[parity], nl_count(c, parity))
                    ins = None
                    for kk in range(compared_by_dve(c, g), L):
                        k = g * L + kk
                        ins = nc.scalar.activation(pos[slot(c, g)][:, kk, :], nl[parity], ACT.Sign, scale=-1.0,
                                                   bias=r_col[:, k:k + 1])
                    if ins is not None:
                        ins.then_inc(signs_ready, 1)
                    if number and c == 0 and g == 0:
                        heads(g)
                        last[4]()
                    if number and c == 0 and g in (2, 6):
                        last[8 if g == 2 else 15]()
                    if g == NC // 2 and not (number and c == 0):
                        relu_rows(c - 1)

            def relu_rows(p):
                act.wait_ge(summed_read, p + 1)
                nc.scalar.activation(y, y, ACT.Relu).then_inc(y_relu, 1)

            def scale_rows(p):
                for t in range(L):
                    act.wait_ge(rows_summed, p * L + t + 1)
                    if not (isinstance(p, int) and p == 0 and t < 2):
                        act.wait_ge(rows_taken, p * L + t - 1)
                    nc.scalar.activation(neg_part[:, t % 2, :], ps[:, 2 * t, 0:GW], ACT.Copy,
                                         scale=cols(b_col, p * L + t, 1)).then_inc(neg_scaled, 1)
            chunked(act, edges)
            scale_rows(NC - 1)

        @block.vector
        def _(dve):
            v = nc.vector
            step = Steps(dve, dve_step)

            def affine0(l):
                dve.wait_ge(rstd0_ready, l + 1)
                v.scalar_tensor_tensor(out=cols_l(sv[:, 3, :], l), in0=by_l(mv0, l)[:, :, 0], scalar=-1.0,
                                       in1=cols_l(sv[:, 2, :], l), op0=ALU.mult, op1=ALU.mult).then_inc(
                    affine_ready, 1)

            for l in range(L):
                dve.wait_ge(x_in_sem[l], 16 * NQ)
                ks = range(l, NK, L)
                for k in ks:
                    ins = v.bn_stats(stats0[:, k, :], x_in[:, k, :])
                if l >= 1:
                    affine0(l - 1)
                step(ins)
                for k in ks:
                    ins = v.bn_aggr(mv0[:, k, :], stats0[:, k, :])
                step(ins)
                v.tensor_scalar(cols_l(sv[:, 0, :], l), by_l(mv0, l)[:, :, 1], LN_EPS, None, ALU.add).then_inc(
                    var0_ready, 1)
                if l == 1:
                    dve.wait_ge(bias_tanh, 1)
                    step(v.scalar_tensor_tensor(out=post[:, 4:5], in0=post[:, 2:3], scalar=MAX_NORM,
                                                in1=post[:, 3:4], op0=ALU.min, op1=ALU.mult))
                    v.tensor_scalar(hb_colv, b_colv, post[:, 4:5], None, ALU.mult).then_inc(bias_ready, 1)
                if l == 0:
                    dve.wait_ge(weights_in, 16 * 3)
                    step(v.tensor_tensor(b_sq, bias_b, bias_b, ALU.mult))
                    step(v.reduce_sum(post[:, 0:1], b_sq, AX_X))
                    v.tensor_scalar(post[:, 0:1], post[:, 0:1], MIN_NORM2, None, ALU.max).then_inc(bias_summed, 1)
            affine0(L - 1)
            step(v.tensor_scalar(hb, bias_b, post[:, 4:5], None, ALU.mult))
            step(v.tensor_tensor(b_sq, hb, hb, ALU.mult))
            step(v.reduce_sum(post[:, 5:6], b_sq, AX_X))
            b2 = post[:, 5:6]

            def turn_block(c, k):
                g, l = k // L, k % L
                if l == 0:
                    dve.wait_ge(adj_in[g % XSLOTS], c * (16 * NQ * NC // XSLOTS) + 16 * NQ * (g // XSLOTS + 1))
                if not (isinstance(c, int) and c == 0 and k < TSLOTS):
                    dve.wait_ge(block_multiplied, c * NK + k - TSLOTS + 1)
                    if k % HB == 0:
                        dve.wait_ge(half_signed, c * TH + (k - TSLOTS) // HB + 1)
                v.transpose(
                    turned[:, k % TSLOTS, :].rearrange("p (l b i) -> p b l i", l=L, b=NQ),
                    loaded[:, g % XSLOTS, :, l * Q:(l + 1) * Q].rearrange("p (b l) q -> p b l q", b=NQ)).then_inc(
                    block_turned, 1)

            for u in range(NG + 2):
                if u < NG:
                    l, j, ks = groups[u]
                    dve.wait_ge(h_squared, u + 1)
                    v.reduce_sum(cols_l(sv[:, 5, :], l, j), by_l(x_in, l, j), AX_X)
                if NG - TSLOTS <= u < NG:
                    turn_block(0, u - (NG - TSLOTS))
                if u >= 2:
                    l, j, ks = groups[u - 2]
                    if u % 2 == 0:
                        dve.wait_ge(mx_squared, u // 2)
                    else:
                        dve.wait_ge(mx_copied, u - 1)
                        dve.wait_ge(h_squared, u - 1)
                        got = by_l(mx, l, j)[:, :, 0:D]
                        step(v.tensor_tensor(by_l(h, l, j), got, got, ALU.mult))
                    ins = v.reduce_sum(cols_l(sv[:, 6, :], l, j), by_l(h, l, j), AX_X)
            step(ins)

            HN, MN, P1, X2, T1, T2 = (sv[:, n, :] for n in (5, 6, 10, 12, 13, 14))
            MB = mx[:, :, D]
            def artanh_over(n, inv, dst, cap, asked):
                lo, hi = sv[:, 8, :], sv[:, 9, :]
                p, q, s, m = sv[:, 15, :], sv[:, 20, :], sv[:, 21, :], sv[:, 22, :]
                step(v.tensor_scalar(p, n, cap, None, ALU.min))
                v.tensor_scalar(lo, p, 1.0, None, ALU.add)
                v.tensor_scalar(hi, p, -1.0, 1.0, ALU.mult, ALU.add).then_inc(act_asked, 1)
                step(v.tensor_tensor(q, p, p, ALU.mult))
                step(v.tensor_scalar(s, q, 1.0 / 13, None, ALU.mult))
                for c in (1 / 11, 1 / 9, 1 / 7, 1 / 5, 1 / 3):
                    step(v.scalar_tensor_tensor(out=s, in0=s, scalar=c, in1=q, op0=ALU.add, op1=ALU.mult))
                v.tensor_scalar(m, p, 0.3, None, ALU.is_lt)
                step(v.scalar_tensor_tensor(out=s, in0=s, scalar=1.0, in1=p, op0=ALU.add, op1=ALU.mult))
                dve.wait_ge(act_done, asked)
                step(v.tensor_tensor(lo, lo, hi, ALU.subtract))
                step(v.scalar_tensor_tensor(out=s, in0=lo, scalar=-0.5, in1=s, op0=ALU.mult, op1=ALU.add))
                step(v.tensor_tensor(s, s, m, ALU.mult))
                step(v.scalar_tensor_tensor(out=lo, in0=lo, scalar=0.5, in1=s, op0=ALU.mult, op1=ALU.add))
                step(v.tensor_tensor(dst, lo, inv, ALU.mult))

            v.tensor_scalar(sv[:, 5:7, :], sv[:, 5:7, :], MIN_NORM2, None, ALU.max).then_inc(roots_asked, 1)
            dve.wait_ge(roots_done, 1)
            step(v.reciprocal(sv[:, 24:26, :], sv[:, 5:7, :]))
            artanh_over(HN, sv[:, 24, :], T1, ARTANH_CLIP, 1)
            v.tensor_tensor(sv[:, 11, :], T1, MN, ALU.mult).then_inc(act_asked, 1)
            dve.wait_ge(act_done, 2)
            step(v.tensor_scalar(P1, sv[:, 11, :], MAX_NORM, None, ALU.min))
            step(v.tensor_tensor(X2, P1, P1, ALU.mult))
            step(v.tensor_tensor(P1, P1, sv[:, 25, :], ALU.mult))
            XY = sv[:, 16, :]
            step(v.tensor_tensor(XY, P1, MB, ALU.mult))
            step(v.tensor_scalar(XY, XY, 2.0, 1.0, ALU.mult, ALU.add))
            A, B, DEN = sv[:, 17, :], sv[:, 18, :], sv[:, 19, :]
            v.tensor_scalar(A, XY, b2, None, ALU.add)
            v.tensor_scalar(B, X2, -1.0, 1.0, ALU.mult, ALU.add)
            step(v.scalar_tensor_tensor(out=DEN, in0=X2, scalar=b2, in1=XY, op0=ALU.mult, op1=ALU.add))
            step(v.tensor_scalar(DEN, DEN, 1e-15, None, ALU.max))
            step(v.reciprocal(DEN, DEN))
            v.tensor_tensor(B, B, DEN, ALU.mult)
            step(v.tensor_tensor(A, A, P1, ALU.mult))
            step(v.tensor_tensor(A, A, DEN, ALU.mult))
            step(v.tensor_tensor(T1, MN, A, ALU.mult))
            step(v.tensor_tensor(T1, T1, T1, ALU.mult))
            step(v.tensor_tensor(T2, A, B, ALU.mult))
            step(v.tensor_tensor(T2, T2, MB, ALU.mult))
            step(v.scalar_tensor_tensor(out=T1, in0=T2, scalar=2.0, in1=T1, op0=ALU.mult, op1=ALU.add))
            step(v.tensor_tensor(T2, B, B, ALU.mult))
            step(v.scalar_tensor_tensor(out=HN, in0=T2, scalar=b2, in1=T1, op0=ALU.mult, op1=ALU.add))
            v.tensor_scalar(HN, HN, MIN_NORM2, None, ALU.max).then_inc(roots_asked, 1)
            dve.wait_ge(roots_done, 2)
            step(v.reciprocal(sv[:, 24, :], HN))
            artanh_over(HN, sv[:, 24, :], T1, MAX_NORM, 3)
            v.tensor_tensor(T2, B, T1, ALU.mult)
            v.tensor_tensor(T1, A, T1, ALU.mult).then_inc(tangent_scales, 1)
            dve.wait_ge(tangent_scales, 1)
            def tangent(k):
                dve.wait_ge(fb_ready, k + 1)
                v.scalar_tensor_tensor(out=xt[:, k, :], in0=mx[:, k, 0:D], scalar=T1[:, k:k + 1],
                                       in1=fb[:, k % XT_AHEAD, :], op0=ALU.mult, op1=ALU.add).then_inc(xt_ready, 1)

            POST = 6

            def post_steps(p):
                first = isinstance(p, int) and p == 0
                chain = Steps(dve, dve_step, p * POST + step.n)
                UI, RN, INV, F, VN, TH_, TF, CO = (post[:, a:b] for a, b in (
                    (8, 12), (12, 16), (16, 20), (20, 24), (24, 28), (28, 32), (32, 36), (56, 60)))

                def relu():
                    dve.wait_ge(support_turned, p + 1)
                    v.tensor_scalar(relu_u[:], support, 0.0, None, ALU.max).then_inc(relu_ready, 1)

                def sums_u():
                    dve.wait_ge(u_squared, p + 1)
                    v.reduce_sum(post[:, 0:4], sq1, AX_X)

                def sums_relu():
                    dve.wait_ge(relu_squared, p + 1)
                    chain(v.reduce_sum(post[:, 4:8], sq2, AX_X))
                    v.tensor_scalar(post[:, 0:8], post[:, 0:8], MIN_NORM2, None, ALU.max).then_inc(sums_ready, 1)

                def shrink():
                    dve.wait_ge(norms_ready, p + 1)
                    chain(v.tensor_scalar(F, UI, ARTANH_RIM, 1.0, ALU.mult, ALU.min))
                    v.tensor_tensor(VN, F, RN, ALU.mult).then_inc(shrunk_ready, 1)

                def coefficient():
                    dve.wait_ge(tanh_ready, p + 1)
                    v.reciprocal(INV, VN)
                    chain(v.scalar_tensor_tensor(out=TF, in0=TH_, scalar=MAX_NORM, in1=F, op0=ALU.min, op1=ALU.mult))
                    chain(v.tensor_tensor(CO, TF, INV, ALU.mult))

                def residual(ls):
                    if ls[0] == 0:
                        dve.wait_ge(xk_loaded, p * (16 * NQ) + 16 * NQ)
                    for l in ls:
                        ins = v.scalar_tensor_tensor(out=xk[:, l, :], in0=relu_u[:, l, :], scalar=CO[:, l:l + 1],
                                                     in1=xk[:, l, :], op0=ALU.mult, op1=ALU.add)
                    if ls[-1] == L - 1:
                        ins.then_inc(x1_ready, 1)

                def spread(ls):
                    if ls[0] == 0:
                        dve.wait_ge(x1_ready, p + 1)
                    for l in ls:
                        ins = v.bn_stats(stats[:, l, :], xk[:, l, :])
                    if ls[-1] == L - 1:
                        chain(ins)

                def variance():
                    v.memset(post[:, 61:62], 0.0)
                    for l in range(L):
                        ins = v.bn_aggr(mv[:, l, :], stats[:, l, :])
                    chain(ins)
                    v.tensor_scalar(post[:, 40:44], mv[:, :, 1], LN_EPS, None, ALU.add).then_inc(var_ready, 1)

                def affine():
                    dve.wait_ge(std_ready, p + 1)
                    if not first:
                        dve.wait_ge(h2_ready, p)
                    v.scalar_tensor_tensor(out=post[:, 36:40], in0=mv[:, :, 0], scalar=-1.0, in1=post[:, 48:52],
                                           op0=ALU.mult, op1=ALU.mult).then_inc(norm2_ready, 1)
                return {7: relu, 12: sums_u, 13: sums_relu, 17: shrink, 20: coefficient,
                        21: lambda: residual((0, 1)), 22: lambda: residual((2, 3)), 23: lambda: spread((0, 1)),
                        24: lambda: spread((2, 3)), 25: variance, 29: affine}


            def turn(c, parity):
                number = isinstance(c, int)
                steps = {} if number and c == 0 else post_steps(c - 1)
                for k in range(NK):
                    if not (number and c == 0 and k < TSLOTS):
                        turn_block(c, k)
                    if number and c == 0:
                        tangent(k)
                    if k in steps:
                        steps[k]()
            chunked(dve, turn)
            last = [f for _, f in sorted(post_steps(NC - 1).items())]
            def compare(c, parity, g):
                if isinstance(c, int) and c == 0 and g == 0:
                    dve.wait_ge(block_multiplied, (NC - 1) * NK + NK // 2)
                    dve.wait_ge(nl_loaded[0], 16)
                else:
                    dve.wait_ge(edges_ready, c * NC + g + 1)
                for kk in range(compared_by_dve(c, g)):
                    k = g * L + kk
                    ins = v.tensor_scalar(pos[slot(c, g)][:, kk, :], nl[parity], r_col[:, k:k + 1], -1.0,
                                          ALU.is_le, ALU.add)
                ins.then_inc(compared, 1)

            compare(0, 0, 0)
            dve.wait_ge(block_multiplied, NC * NK)
            dve.wait_ge(half_signed, NC * TH)
            dve.wait_ge(factors_ready, 1)
            for w, s_col in ((0, s0_col), (1, s1_col)):
                ins = v.tensor_copy(G[w][:, :, 2 * D], s_col[:])
            ins.then_inc(weight_heads, 1)
            dve.wait_ge(weight_heads, 1)
            for w, s_col in ((0, s0_col), (1, s1_col)):
                ins = v.tensor_tensor(G[w][:, :, 2 * D + 1], s_col[:], G[w][:, :, 2 * D], ALU.subtract)
            ins.then_inc(weight_cols, 1)
            last.pop(0)()

            def rests(g, part):
                first = g * L + part * HB if g else 0
                for k in range(first, g * L + (part + 1) * HB) if g or part else ():
                    dve.wait_ge(head_ready, k + 1)
                    v.scalar_tensor_tensor(out=G[1][:, k, D:2 * D], in0=h2[:, k, :], scalar=s1_col[:, k:k + 1],
                                           in1=G[1][:, k, 0:D], op0=ALU.mult, op1=ALU.subtract).then_inc(
                        rest_ready, 1)

            def split(c, parity):
                number = isinstance(c, int)
                if not (number and c == 0):
                    dve.wait_ge(nl_loaded[parity], nl_count(c, parity))
                ahead = not (number and c == 0)
                if ahead:
                    compare(c, parity, 0)
                for g in range(NC):
                    pos_g, neg_g = pos[slot(c, g)], neg[slot(c, g)]
                    if not ahead and g:
                        compare(c, parity, g)
                    if not ahead:
                        rests(g, 0)
                    dve.wait_ge(edges_ready, c * NC + g + 1)
                    if ahead or g:
                        dve.wait_ge(signs_ready, c * NC + g)
                    dve.wait_ge(compared, c * NC + g + 1)
                    v.tensor_tensor(pos_g, pos_g, neg_g, ALU.add).then_inc(coded, 1)
                    if not ahead:
                        rests(g, 1)
                    rows_at = 0 if number and c == 1 else 1
                    if ahead and g + 1 < NC and not rows_at <= g <= 1:
                        compare(c, parity, g + 1)
                    dve.wait_ge(coded, c * NC + g + 1)
                    v.tensor_scalar(neg_g, pos_g, 3.0, None, ALU.is_equal)
                    v.tensor_scalar(pos_g, pos_g, 4.0, None, ALU.is_ge).then_inc(parts_ready, 1)
                    if not ahead:
                        for _ in range({0: 2, 1: 1, 2: 3, 3: 3, 4: 1}.get(g, 0)):
                            last.pop(0)()
                    if g == rows_at and ahead:
                        take_rows(c - 1)
                    if ahead and g <= 1 and g >= rows_at:
                        compare(c, parity, g + 1)

            def take(p, t):
                if t == 0 and not (isinstance(p, int) and p == 0):
                    dve.wait_ge(summed_read, p)
                dve.wait_ge(neg_scaled, p * L + t + 1)
                v.scalar_tensor_tensor(out=summed[:, t, :], in0=ps[:, 2 * t + 1, 0:GW],
                                       scalar=cols(a_col, p * L + t, 1), in1=neg_part[:, t % 2, :],
                                       op0=ALU.mult, op1=ALU.add).then_inc(rows_taken, 1)

            def take_rows(p):
                for t in range(L):
                    take(p, t)
                dve.wait_ge(rows_taken, p * L + L)
                v.tensor_tensor(post[:, 56:60], summed[:, :, 2 * D], summed[:, :, 2 * D + 1], ALU.add).then_inc(
                    weights_summed, 1)
                dve.wait_ge(weights_summed, p + 1)
                v.reciprocal(post[:, 52:56], post[:, 56:60]).then_inc(recip_ready, 1)

            chunked(dve, split)
            final = Steps(dve, final_step)
            for l in range(0, L, 2):
                take(NC - 1, l)
                take(NC - 1, l + 1)
                if l == 0:
                    dve.wait_ge(out_stored, (NC - 1) * (16 * NQ))
                two = slice(l, l + 2)
                dve.wait_ge(rows_taken, (NC - 1) * L + l + 2)
                v.tensor_tensor(post[:, 56 + l:58 + l], summed[:, two, 2 * D], summed[:, two, 2 * D + 1], ALU.add)
                final(v.tensor_tensor(y[:, two], summed[:, two, 0:D], summed[:, two, D:2 * D], ALU.add))
                final(v.reciprocal(post[:, 52 + l:54 + l], post[:, 56 + l:58 + l]))
                for n in (l, l + 1):
                    ins = v.tensor_scalar(y[:, n], y[:, n], post[:, 52 + n:53 + n], 0.0, ALU.mult, ALU.max)
                final(ins)
                dve.wait_ge(x1_loaded, NC * (16 * NQ))
                v.tensor_tensor(y[:, two], y[:, two], x1k[:, two], ALU.add).then_inc(y_ready, 1)


_INS = ['x', 'adj', 'L0_gnn_weight', 'L0_gnn_bias', 'L1_gnn_context', 'L1_gnn_W_common', 'L1_gnn_w_left',
        'L1_gnn_b_left', 'L1_gnn_w_right', 'L1_gnn_b_right']
_OUTS = [((4096, 128), 'float32')]


def kernel(**inputs):
    import numpy as _np
    import concourse.bacc as _bacc
    from concourse import mybir as _mybir
    from concourse.bass_utils import run_bass_kernel_spmd as _run

    nc = _bacc.Bacc("TRN2", target_bir_lowering=False, num_devices=1)
    arrays, args = {}, []
    for name in _INS:
        a = _np.ascontiguousarray(inputs[name])
        if a.ndim == 0 or name.endswith(("b_left", "b_right")):
            a = a.reshape(1, 1)
        arrays[f"in_{name}_dram"] = a
        args.append(nc.dram_tensor(f"in_{name}_dram", a.shape, _mybir.dt.from_np(a.dtype), kind="ExternalInput").ap())
    for i, (shape, dtype) in enumerate(_OUTS):
        dt = _mybir.dt.from_np(_np.dtype(dtype))
        args.append(nc.dram_tensor(f"out_{i}_dram", shape, dt, kind="ExternalOutput").ap())
    bass_two_graph_layers(nc, *args)
    r = _run(nc, [arrays], core_ids=[0])
    return r.results[0]["out_0_dram"]
```
